# Optimizing a Trainium2 kernel written in Bass

```python
import numpy as np
import jax
import jax.numpy as jnp

def _softmax(x, axis=-1):
    return jax.nn.softmax(x, axis=axis)

def _gelu(x):
    return jax.nn.gelu(x, approximate=True)

def _silu(x):
    return jax.nn.silu(x)

def _sigmoid(x):
    return jax.nn.sigmoid(x)

def _layernorm(x, axis=-1, eps=1e-05):
    m = jnp.mean(x, axis=axis, keepdims=True)
    v = jnp.var(x, axis=axis, keepdims=True)
    return (x - m) / jnp.sqrt(v + eps)

def _scatter_add(tgt, idx, src, axis=0):
    return tgt.at[idx].add(src)

def _segment_sum(src, seg, n):
    return jax.ops.segment_sum(src, seg, n)
kernel_name = 'mk_hybrid_d1_jaxref_r8_20dd0f'

def setup_inputs(seed: int=0):
    np.random.seed(seed)
    _w = jnp.asarray

    def _L0_attn_a_setup():
        import jax, jax.numpy as jnp
        import numpy as np
        from jax import lax
        N_HEADS = 16
        EPS = 1e-06
        CHUNK = 128

        def causal_dot_product(q, k, v):
            B, H, L, D = q.shape
            M = v.shape[-1]
            nc = L // CHUNK
            qc = q.reshape(B, H, nc, CHUNK, D).transpose(2, 0, 1, 3, 4)
            kc = k.reshape(B, H, nc, CHUNK, D).transpose(2, 0, 1, 3, 4)
            vc = v.reshape(B, H, nc, CHUNK, M).transpose(2, 0, 1, 3, 4)

            def step(kv_carry, inp):
                qb, kb, vb = inp
                kv = jnp.einsum('bhcd,bhcm->bhcdm', kb, vb)
                kv_cum = jnp.cumsum(kv, axis=2) + kv_carry[:, :, None]
                out = jnp.einsum('bhcd,bhcdm->bhcm', qb, kv_cum)
                return (kv_cum[:, :, -1], out)
            init = jnp.zeros((B, H, D, M), q.dtype)
            _, outs = lax.scan(step, init, (qc, kc, vc))
            return outs.transpose(1, 2, 0, 3, 4).reshape(B, H, L, M)

        def flow_attention_causal(x, Wq, bq, Wk, bk, Wv, bv, Wo, bo):
            B, L, _ = x.shape
            d_model = Wq.shape[1]
            H = N_HEADS
            q = (x @ Wq + bq).reshape(B, L, H, -1).transpose(0, 2, 1, 3)
            k = (x @ Wk + bk).reshape(B, L, H, -1).transpose(0, 2, 1, 3)
            v = (x @ Wv + bv).reshape(B, L, H, -1).transpose(0, 2, 1, 3)
            q = jax.nn.sigmoid(q)
            k = jax.nn.sigmoid(k)
            sink_incoming = 1.0 / jnp.einsum('bhld,bhld->bhl', q + EPS, jnp.cumsum(k, axis=2) + EPS)
            source_outgoing = 1.0 / jnp.einsum('bhld,bhld->bhl', k + EPS, jnp.cumsum(q, axis=2) + EPS)
            normal = (jnp.arange(L, dtype=x.dtype) + 1.0)[None, None, :]
            sink_incoming = sink_incoming * normal
            source_outgoing = source_outgoing * normal
            conserved_sink = jnp.einsum('bhld,bhld->bhl', q + EPS, jnp.cumsum(k * source_outgoing[..., None], axis=2) + EPS) / normal
            conserved_source = jnp.einsum('bhld,bhld->bhl', k + EPS, jnp.cumsum(q * sink_incoming[..., None], axis=2) + EPS) / normal
            sink_allocation = jax.nn.sigmoid(conserved_sink)
            cs = jnp.exp(conserved_source)
            source_competition = cs / jnp.cumsum(cs, axis=-1) * normal
            out = causal_dot_product(q * (sink_incoming / normal)[..., None], k, v * source_competition[..., None]) * sink_allocation[..., None]
            out = out.transpose(0, 2, 1, 3).reshape(B, L, d_model)
            return out @ Wo + bo
        key = jax.random.key(seed)
        ks = jax.random.split(key, 9)
        B, L, d_model = (4, 512, 128)
        s = 0.02
        return {'x': jax.random.normal(ks[0], (B, L, d_model), dtype=jnp.float32), 'Wq': jax.random.normal(ks[1], (d_model, d_model), dtype=jnp.float32) * s, 'bq': jnp.zeros((d_model,), dtype=jnp.float32), 'Wk': jax.random.normal(ks[2], (d_model, d_model), dtype=jnp.float32) * s, 'bk': jnp.zeros((d_model,), dtype=jnp.float32), 'Wv': jax.random.normal(ks[3], (d_model, d_model), dtype=jnp.float32) * s, 'bv': jnp.zeros((d_model,), dtype=jnp.float32), 'Wo': jax.random.normal(ks[4], (d_model, d_model), dtype=jnp.float32) * s, 'bo': jnp.zeros((d_model,), dtype=jnp.float32)}
    _L0_attn_a_in = _L0_attn_a_setup()

    def _L0_attn_b_setup():
        import jax, jax.numpy as jnp
        import numpy as np
        B, S, D, H = (2, 256, 128, 16)
        HD = D // H
        SCALE = 1.0 / np.sqrt(HD)
        key = jax.random.key(seed)
        k1, k2, k3, k4, k5 = jax.random.split(key, 5)
        return {'hidden_states': jax.random.normal(k1, (B, S, D), dtype=jnp.float32), 'c_attn_w': jax.random.normal(k2, (D, 3 * D), dtype=jnp.float32) * 0.02, 'c_attn_b': jax.random.normal(k3, (3 * D,), dtype=jnp.float32) * 0.02, 'c_proj_w': jax.random.normal(k4, (D, D), dtype=jnp.float32) * 0.02, 'c_proj_b': jax.random.normal(k5, (D,), dtype=jnp.float32) * 0.02}
    _L0_attn_b_in = _L0_attn_b_setup()

    def _L0_ffn_setup():
        import jax, jax.numpy as jnp
        import numpy as np
        H = 128
        I = 88
        E = 64
        TOP_K = 8
        NG = 8
        TOPK_GROUP = 4
        N_SHARED = 2
        ROUTED_SCALE = 2.5
        S_I = I * N_SHARED

        def _route(x, gate_w, gate_bias):
            T = x.shape[0]
            logits = x @ gate_w.T
            scores = jax.nn.sigmoid(logits)
            scores_for_choice = scores + gate_bias[None, :]
            grp = scores_for_choice.reshape(T, NG, E // NG)
            group_scores = jnp.sum(jax.lax.top_k(grp, 2)[0], axis=-1)
            _, gidx = jax.lax.top_k(group_scores, TOPK_GROUP)
            gmask = jnp.zeros((T, NG), dtype=scores.dtype).at[jnp.arange(T)[:, None], gidx].set(1.0)
            emask = jnp.repeat(gmask, E // NG, axis=1)
            masked = jnp.where(emask > 0, scores_for_choice, 0.0)
            _, topk_idx = jax.lax.top_k(masked, TOP_K)
            topk_w = jnp.take_along_axis(scores, topk_idx, axis=1)
            topk_w = topk_w / (jnp.sum(topk_w, axis=-1, keepdims=True) + 1e-20)
            topk_w = topk_w * ROUTED_SCALE
            rw = jnp.zeros((T, E), dtype=scores.dtype).at[jnp.arange(T)[:, None], topk_idx].add(topk_w)
            return rw

        def _mlp(x, gw, uw, dw):
            return jax.nn.silu(x @ gw.T) * (x @ uw.T) @ dw.T
        key = jax.random.key(seed)
        ks = jax.random.split(key, 10)
        sc = 0.02
        return {'hidden_states': jax.random.normal(ks[0], (1, 128, H), dtype=jnp.float32), 'gate_w': sc * jax.random.normal(ks[1], (E, H), dtype=jnp.float32), 'gate_bias': sc * jax.random.normal(ks[2], (E,), dtype=jnp.float32), 'Wg': sc * jax.random.normal(ks[3], (E, I, H), dtype=jnp.float32), 'Wu': sc * jax.random.normal(ks[4], (E, I, H), dtype=jnp.float32), 'Wd': sc * jax.random.normal(ks[5], (E, H, I), dtype=jnp.float32), 'Sg': sc * jax.random.normal(ks[6], (S_I, H), dtype=jnp.float32), 'Su': sc * jax.random.normal(ks[7], (S_I, H), dtype=jnp.float32), 'Sd': sc * jax.random.normal(ks[8], (H, S_I), dtype=jnp.float32)}
    _L0_ffn_in = _L0_ffn_setup()
    _d = {'L0_attn_a_x': _L0_attn_a_in['x'], 'L0_attn_a_Wq': _L0_attn_a_in['Wq'], 'L0_attn_a_bq': _L0_attn_a_in['bq'], 'L0_attn_a_Wk': _L0_attn_a_in['Wk'], 'L0_attn_a_bk': _L0_attn_a_in['bk'], 'L0_attn_a_Wv': _L0_attn_a_in['Wv'], 'L0_attn_a_bv': _L0_attn_a_in['bv'], 'L0_attn_a_Wo': _L0_attn_a_in['Wo'], 'L0_attn_a_bo': _L0_attn_a_in['bo'], 'L0_attn_b_c_attn_w': _L0_attn_b_in['c_attn_w'], 'L0_attn_b_c_attn_b': _L0_attn_b_in['c_attn_b'], 'L0_attn_b_c_proj_w': _L0_attn_b_in['c_proj_w'], 'L0_attn_b_c_proj_b': _L0_attn_b_in['c_proj_b'], 'L0_ffn_gate_w': _L0_ffn_in['gate_w'], 'L0_ffn_gate_bias': _L0_ffn_in['gate_bias'], 'L0_ffn_Wg': _L0_ffn_in['Wg'], 'L0_ffn_Wu': _L0_ffn_in['Wu'], 'L0_ffn_Wd': _L0_ffn_in['Wd'], 'L0_ffn_Sg': _L0_ffn_in['Sg'], 'L0_ffn_Su': _L0_ffn_in['Su'], 'L0_ffn_Sd': _L0_ffn_in['Sd']}
    _x0 = _d['L0_attn_a_x']
    _d['L0_attn_a_x'] = jax.random.normal(jax.random.fold_in(jax.random.key(seed), 1), (16, 256, 128), dtype=_x0.dtype)
    del _x0
    return _d

def reference(L0_attn_a_x, L0_attn_a_Wq, L0_attn_a_bq, L0_attn_a_Wk, L0_attn_a_bk, L0_attn_a_Wv, L0_attn_a_bv, L0_attn_a_Wo, L0_attn_a_bo, L0_attn_b_c_attn_w, L0_attn_b_c_attn_b, L0_attn_b_c_proj_w, L0_attn_b_c_proj_b, L0_ffn_gate_w, L0_ffn_gate_bias, L0_ffn_Wg, L0_ffn_Wu, L0_ffn_Wd, L0_ffn_Sg, L0_ffn_Su, L0_ffn_Sd):

    def _L0_attn_a_ref(x, Wq, bq, Wk, bk, Wv, bv, Wo, bo):
        import jax, jax.numpy as jnp
        import numpy as np
        from jax import lax
        N_HEADS = 16
        EPS = 1e-06
        CHUNK = 128

        def causal_dot_product(q, k, v):
            B, H, L, D = q.shape
            M = v.shape[-1]
            nc = L // CHUNK
            qc = q.reshape(B, H, nc, CHUNK, D).transpose(2, 0, 1, 3, 4)
            kc = k.reshape(B, H, nc, CHUNK, D).transpose(2, 0, 1, 3, 4)
            vc = v.reshape(B, H, nc, CHUNK, M).transpose(2, 0, 1, 3, 4)

            def step(kv_carry, inp):
                qb, kb, vb = inp
                kv = jnp.einsum('bhcd,bhcm->bhcdm', kb, vb)
                kv_cum = jnp.cumsum(kv, axis=2) + kv_carry[:, :, None]
                out = jnp.einsum('bhcd,bhcdm->bhcm', qb, kv_cum)
                return (kv_cum[:, :, -1], out)
            init = jnp.zeros((B, H, D, M), q.dtype)
            _, outs = lax.scan(step, init, (qc, kc, vc))
            return outs.transpose(1, 2, 0, 3, 4).reshape(B, H, L, M)

        def flow_attention_causal(x, Wq, bq, Wk, bk, Wv, bv, Wo, bo):
            B, L, _ = x.shape
            d_model = Wq.shape[1]
            H = N_HEADS
            q = (x @ Wq + bq).reshape(B, L, H, -1).transpose(0, 2, 1, 3)
            k = (x @ Wk + bk).reshape(B, L, H, -1).transpose(0, 2, 1, 3)
            v = (x @ Wv + bv).reshape(B, L, H, -1).transpose(0, 2, 1, 3)
            q = jax.nn.sigmoid(q)
            k = jax.nn.sigmoid(k)
            sink_incoming = 1.0 / jnp.einsum('bhld,bhld->bhl', q + EPS, jnp.cumsum(k, axis=2) + EPS)
            source_outgoing = 1.0 / jnp.einsum('bhld,bhld->bhl', k + EPS, jnp.cumsum(q, axis=2) + EPS)
            normal = (jnp.arange(L, dtype=x.dtype) + 1.0)[None, None, :]
            sink_incoming = sink_incoming * normal
            source_outgoing = source_outgoing * normal
            conserved_sink = jnp.einsum('bhld,bhld->bhl', q + EPS, jnp.cumsum(k * source_outgoing[..., None], axis=2) + EPS) / normal
            conserved_source = jnp.einsum('bhld,bhld->bhl', k + EPS, jnp.cumsum(q * sink_incoming[..., None], axis=2) + EPS) / normal
            sink_allocation = jax.nn.sigmoid(conserved_sink)
            cs = jnp.exp(conserved_source)
            source_competition = cs / jnp.cumsum(cs, axis=-1) * normal
            out = causal_dot_product(q * (sink_incoming / normal)[..., None], k, v * source_competition[..., None]) * sink_allocation[..., None]
            out = out.transpose(0, 2, 1, 3).reshape(B, L, d_model)
            return out @ Wo + bo
        return flow_attention_causal(x, Wq, bq, Wk, bk, Wv, bv, Wo, bo)

    def _L0_attn_b_ref(hidden_states, c_attn_w, c_attn_b, c_proj_w, c_proj_b):
        import jax, jax.numpy as jnp
        import numpy as np
        B, S, D, H = (2, 256, 128, 16)
        HD = D // H
        SCALE = 1.0 / np.sqrt(HD)
        b, s, d = hidden_states.shape
        qkv = hidden_states @ c_attn_w + c_attn_b
        q, k, v = jnp.split(qkv, 3, axis=-1)

        def heads(t):
            return t.reshape(b, s, H, HD).transpose(0, 2, 1, 3)
        q, k, v = (heads(q), heads(k), heads(v))
        scores = jnp.einsum('bhqd,bhkd->bhqk', q, k) * SCALE
        causal = jnp.tril(jnp.ones((s, s), dtype=bool))
        mask_value = jnp.finfo(scores.dtype).min
        scores = jnp.where(causal[None, None], scores, mask_value)
        attn = jax.nn.softmax(scores, axis=-1)
        out = jnp.einsum('bhqk,bhkd->bhqd', attn, v)
        out = out.transpose(0, 2, 1, 3).reshape(b, s, d)
        out = out @ c_proj_w + c_proj_b
        return out

    def _L0_ffn_ref(hidden_states, gate_w, gate_bias, Wg, Wu, Wd, Sg, Su, Sd):
        import jax, jax.numpy as jnp
        import numpy as np
        H = 128
        I = 88
        E = 64
        TOP_K = 8
        NG = 8
        TOPK_GROUP = 4
        N_SHARED = 2
        ROUTED_SCALE = 2.5
        S_I = I * N_SHARED

        def _route(x, gate_w, gate_bias):
            T = x.shape[0]
            logits = x @ gate_w.T
            scores = jax.nn.sigmoid(logits)
            scores_for_choice = scores + gate_bias[None, :]
            grp = scores_for_choice.reshape(T, NG, E // NG)
            group_scores = jnp.sum(jax.lax.top_k(grp, 2)[0], axis=-1)
            _, gidx = jax.lax.top_k(group_scores, TOPK_GROUP)
            gmask = jnp.zeros((T, NG), dtype=scores.dtype).at[jnp.arange(T)[:, None], gidx].set(1.0)
            emask = jnp.repeat(gmask, E // NG, axis=1)
            masked = jnp.where(emask > 0, scores_for_choice, 0.0)
            _, topk_idx = jax.lax.top_k(masked, TOP_K)
            topk_w = jnp.take_along_axis(scores, topk_idx, axis=1)
            topk_w = topk_w / (jnp.sum(topk_w, axis=-1, keepdims=True) + 1e-20)
            topk_w = topk_w * ROUTED_SCALE
            rw = jnp.zeros((T, E), dtype=scores.dtype).at[jnp.arange(T)[:, None], topk_idx].add(topk_w)
            return rw

        def _mlp(x, gw, uw, dw):
            return jax.nn.silu(x @ gw.T) * (x @ uw.T) @ dw.T
        B, S, _ = hidden_states.shape
        x = hidden_states.reshape(B * S, H)
        rw = _route(x, gate_w, gate_bias)
        expert_out = jax.vmap(lambda gw_, uw_, dw_: _mlp(x, gw_, uw_, dw_))(Wg, Wu, Wd)
        routed = jnp.einsum('eth,te->th', expert_out, rw)
        shared = _mlp(x, Sg, Su, Sd)
        out = (routed + shared).reshape(B, S, H)
        return out
    x = L0_attn_a_x
    x = x + _L0_attn_a_ref(_layernorm(x, axis=-1), L0_attn_a_Wq, L0_attn_a_bq, L0_attn_a_Wk, L0_attn_a_bk, L0_attn_a_Wv, L0_attn_a_bv, L0_attn_a_Wo, L0_attn_a_bo)
    x = x + _L0_ffn_ref(_layernorm(x, axis=-1), L0_ffn_gate_w, L0_ffn_gate_bias, L0_ffn_Wg, L0_ffn_Wu, L0_ffn_Wd, L0_ffn_Sg, L0_ffn_Su, L0_ffn_Sd)
    x = x + _L0_attn_b_ref(_layernorm(x, axis=-1), L0_attn_b_c_attn_w, L0_attn_b_c_attn_b, L0_attn_b_c_proj_w, L0_attn_b_c_proj_b)
    x = x + _L0_ffn_ref(_layernorm(x, axis=-1), L0_ffn_gate_w, L0_ffn_gate_bias, L0_ffn_Wg, L0_ffn_Wu, L0_ffn_Wd, L0_ffn_Sg, L0_ffn_Su, L0_ffn_Sd)
    return x

_drawn_inputs = setup_inputs


def setup_inputs(seed=0):
    import zlib

    import numpy as np

    out = dict(_drawn_inputs(seed))
    spreads = {'L0_attn_a_bq': (0.0, 0.8),
     'L0_attn_a_bk': (0.0, 0.8),
     'L0_attn_a_bv': (0.0, 0.419),
     'L0_attn_a_bo': (0.0, 0.1)}
    factors = {'L0_attn_a_Wq': 8.0,
     'L0_attn_a_Wk': 8.0,
     'L0_attn_a_Wv': 8.0,
     'L0_attn_a_Wo': 2.739,
     'L0_attn_b_c_attn_w': 5.899,
     'L0_attn_b_c_attn_b': 8.0,
     'L0_attn_b_c_proj_w': 5.647,
     'L0_attn_b_c_proj_b': 2.785,
     'L0_ffn_gate_w': 7.209,
     'L0_ffn_gate_bias': 8.0,
     'L0_ffn_Wg': 6.652,
     'L0_ffn_Wu': 6.619,
     'L0_ffn_Wd': 6.621,
     'L0_ffn_Sg': 4.2,
     'L0_ffn_Su': 4.208,
     'L0_ffn_Sd': 4.187}
    for name, (base, spread) in spreads.items():
        noise = np.random.default_rng([zlib.crc32(name.encode()), seed]).standard_normal(out[name].shape)
        drawn = base * np.exp(spread * noise) if base else spread * noise
        out[name] = jnp.asarray(drawn.astype(out[name].dtype))
    for name, factor in factors.items():
        out[name] = (out[name] * factor).astype(out[name].dtype)
    return out
```

```python
from contextlib import ExitStack

import numpy as np

import concourse.bass as bass
from concourse import mybir

F32 = mybir.dt.float32
F32R = mybir.dt.float32r
F16 = mybir.dt.float16
BF16 = mybir.dt.bfloat16
I32 = mybir.dt.int32
ACT = mybir.ActivationFunctionType
ALU = mybir.AluOpType
AX = mybir.AxisListType

P = 128
D = 128
BATCH, SEQ = 16, 256
TOKENS = BATCH * SEQ
TILE = 512
NTILES = TOKENS // TILE
NSUB = TILE // P
HEADS, HD = 16, 8
QUADS = HEADS // 4
EXPERTS, INNER = 64, 88
GROUPS, GSIZE, TOP_GROUPS = 8, 8, 4
ROUTED = EXPERTS * INNER
SHARED = 2 * INNER
RCHUNKS = ROUTED // P
NCHUNKS = RCHUNKS + 2
LN_EPS = 1e-5
FLOW_EPS = 1e-6
NEG = -1.0e30
SCALE = 1.0 / float(np.sqrt(HD))
LOSCALE = 2048.0
NSUBS = TOKENS // P


class Shared:
    pass


def chunk_rows(c):
    return (c * P, P) if c < RCHUNKS else (ROUTED + (c - RCHUNKS) * INNER, INNER)


def layernorm(nc, g, tag, logits):
    with ExitStack() as ctx:
        def sb(n, s, d=F32): return ctx.enter_context(nc.sbuf_tensor(f"{tag}_{n}", s, d))
        def sem(n): return g.ctx.enter_context(nc.semaphore(f"{tag}_{n}"))
        xc, sq, sd, xn = (sb(n, [P, 2, TILE]) for n in ("xc", "sq", "sd", "xn"))
        if logits:
            hi, lo = sb("hi", [P, 2, TILE], F32R), sb("lo", [P, 2, TILE], F32R)
        mean = [g.bank[0], g.bank[1]]
        var = [g.bank[2], g.bank[3]]
        mean_ready, centred, squared, var_ready, sd_ready = (
            sem(n) for n in ("mean_ready", "centred", "squared", "var_ready", "sd_ready"))
        divided, hi_ready, lo_ready, stored, logits_ready = (
            sem(n) for n in ("divided", "hi_ready", "lo_ready", "stored", "logits_ready"))
        stored = [stored, sem("stored_odd")]
        inverted = sem("inverted")
        stores = 2 if logits else 1
        block = ctx.enter_context(nc.Block())

        def route(pe, m):
            pe.wait_ge(divided, m + 1)
            for s in range(NSUB):
                k = m * NSUB + s
                mm = pe.matmul(g.bank[4 + k // 8][:, (k % 8) * EXPERTS:(k % 8 + 1) * EXPERTS],
                               xn[:, m % 2, s * P:(s + 1) * P], g.gate_wT[:], start=True, stop=True)
            mm.then_inc(logits_ready, 1)

        @block.tensor
        def _(pe):
            for n in range(NTILES + 1):
                if n < NTILES:
                    if n >= 2:
                        pe.wait_ge(centred, n - 1)
                    pe.matmul(mean[n % 2], g.ones_d[:], g.x_res[:, n * TILE:(n + 1) * TILE],
                              start=True, stop=True).then_inc(mean_ready, 1)
                if n >= 1:
                    m = n - 1
                    pe.wait_ge(squared, m + 1)
                    if m >= 2:
                        pe.wait_ge(sd_ready, m - 1)
                    pe.matmul(var[m % 2], g.ones_d[:], sq[:, m % 2, :], start=True, stop=True).then_inc(var_ready, 1)
                if logits and n >= 2:
                    route(pe, n - 2)
            if logits:
                route(pe, NTILES - 1)

        @block.vector
        def _(dve):
            for n in range(NTILES + 1):
                if n < NTILES:
                    dve.wait_ge(mean_ready, n + 1)
                    if n >= 2:
                        dve.wait_ge(squared, n - 1)
                        dve.wait_ge(divided, n - 1)
                    dve.tensor_tensor(xc[:, n % 2, :], g.x_res[:, n * TILE:(n + 1) * TILE], mean[n % 2],
                                      ALU.subtract).then_inc(centred, 1)
                if n >= 1:
                    m = n - 1
                    dve.wait_ge(sd_ready, m + 1)
                    dve.wait_ge(centred, m + 1)
                    if m >= 2:
                        if logits:
                            dve.wait_ge(logits_ready, m - 1)
                            dve.wait_ge(hi_ready, m - 1)
                            dve.wait_ge(lo_ready, m - 1)
                        else:
                            dve.wait_ge(stored[m % 2], 16 * (m // 2))
                    dve.reciprocal(sd[:, m % 2, :], sd[:, m % 2, :]).then_inc(inverted, 1)
                    dve.wait_ge(inverted, m + 1)
                    dve.tensor_tensor(xn[:, m % 2, :], xc[:, m % 2, :], sd[:, m % 2, :], ALU.mult).then_inc(divided, 1)
                    if logits:
                        dve.wait_ge(hi_ready, m + 1)
                        dve.wait_ge(divided, m + 1)
                        if m >= 2:
                            dve.wait_ge(stored[m % 2], 32 * (m // 2))
                        dve.tensor_tensor(lo[:, m % 2, :], xn[:, m % 2, :], hi[:, m % 2, :].bitcast(F32),
                                          ALU.subtract).then_inc(lo_ready, 1)

        @block.scalar
        def _(act):
            for n in range(NTILES):
                act.wait_ge(centred, n + 1)
                if n >= 2:
                    act.wait_ge(var_ready, n - 1)
                act.activation(sq[:, n % 2, :], xc[:, n % 2, :], ACT.Square).then_inc(squared, 1)
                act.wait_ge(var_ready, n + 1)
                if n >= 2:
                    act.wait_ge(divided, n - 1)
                act.activation(sd[:, n % 2, :], var[n % 2], ACT.Sqrt, bias=g.ln_eps[:, 0:1]).then_inc(sd_ready, 1)
                if logits:
                    act.wait_ge(divided, n + 1)
                    if n >= 2:
                        act.wait_ge(stored[n % 2], 32 * (n // 2))
                        act.wait_ge(lo_ready, n - 1)
                    act.activation(hi[:, n % 2, :], xn[:, n % 2, :], ACT.Copy).then_inc(hi_ready, 1)

        @block.sync
        def _(sp):
            for n in range(NTILES):
                at = slice(n * TILE, (n + 1) * TILE)
                if logits:
                    sp.wait_ge(hi_ready, n + 1)
                    sp.dma_start(g.xn_hi_dram[:, at], hi[:, n % 2, :].bitcast(F32)).then_inc(stored[n % 2], 16)
                    sp.wait_ge(lo_ready, n + 1)
                    sp.dma_start(g.xn_lo_dram[:, at], lo[:, n % 2, :].bitcast(F32)).then_inc(stored[n % 2], 16)
                else:
                    sp.wait_ge(divided, n + 1)
                    sp.dma_start(g.xn_dram[:, at], xn[:, n % 2, :]).then_inc(stored[n % 2], 16)
            for u in range(2):
                sp.wait_ge(stored[u], 16 * stores * (NTILES // 2))


def routing(nc, g, tag):
    with ExitStack() as ctx:
        def sb(n, s, d=F32): return ctx.enter_context(nc.sbuf_tensor(f"{tag}_{n}", s, d))
        def sem(n): return g.ctx.enter_context(nc.semaphore(f"{tag}_{n}"))
        N = NSUBS * EXPERTS
        scores = sb("scores", [P, N])
        choice = sb("choice", [P, N])
        work = sb("work", [P, N])
        work2 = sb("work2", [P, N])
        halves = choice[:].bitcast(F16).rearrange("p (s e) -> p s e", e=2 * EXPERTS)
        NG = NSUBS * GROUPS
        big1, small1 = sb("big1", [P, NG * 4]), work2
        big2, small2 = sb("big2", [P, NG * 2]), sb("small2", [P, NG * 2])
        mid = sb("mid", [P, NG * 2])
        gscore, rank = sb("gscore", [P, NG]), sb("rank", [P, NG])
        top8 = sb("top8", [P, NSUBS, 8])
        total = sb("total", [P, NSUBS])
        scored, chain, halves_ready, turned, copied = (
            sem(n) for n in ("scored", "chain", "halves_ready", "turned", "copied"))
        sel_zero = sem("sel_zero")
        block = ctx.enter_context(nc.Block())

        @block.scalar
        def _(act):
            for k in range(4):
                i = act.activation(scores[:, k * 512:(k + 1) * 512], g.bank[4 + k], ACT.Sigmoid)
                i.then_inc(scored, 1)
            for k in range(NSUBS // 8):
                act.wait_ge(turned, k + 1)
                act.activation(g.wT[:, k * 1024:(k + 1) * 1024], g.bank[k % 4].bitcast(F16), ACT.Copy).then_inc(copied, 1)

        @block.vector
        def _(dve):
            steps = [0]

            def link(ins):
                steps[0] += 1
                ins.then_inc(chain, 1)
                dve.wait_ge(chain, steps[0])

            dve.wait_ge(scored, 4)
            c3 = choice[:].rearrange("p (s e) -> p s e", e=EXPERTS)
            link(dve.tensor_tensor(c3, scores[:].rearrange("p (s e) -> p s e", e=EXPERTS),
                                   g.gate_bias[:].unsqueeze(1).to_broadcast([P, NSUBS, EXPERTS]), ALU.add))
            pair = choice[:].rearrange("p (n two) -> p n two", two=2)
            link(dve.tensor_tensor(big1[:], pair[:, :, 0], pair[:, :, 1], ALU.max))
            link(dve.tensor_tensor(small1[:, 0:NG * 4], pair[:, :, 0], pair[:, :, 1], ALU.min))
            bp = big1[:].rearrange("p (n two) -> p n two", two=2)
            sp_ = small1[:, 0:NG * 4].rearrange("p (n two) -> p n two", two=2)
            link(dve.tensor_tensor(big2[:], bp[:, :, 0], bp[:, :, 1], ALU.max))
            link(dve.tensor_tensor(mid[:], bp[:, :, 0], bp[:, :, 1], ALU.min))
            link(dve.tensor_tensor(small2[:], sp_[:, :, 0], sp_[:, :, 1], ALU.max))
            link(dve.tensor_tensor(small2[:], small2[:], mid[:], ALU.max))
            bq = big2[:].rearrange("p (n two) -> p n two", two=2)
            sq_ = small2[:].rearrange("p (n two) -> p n two", two=2)
            link(dve.tensor_tensor(gscore[:], bq[:, :, 0], bq[:, :, 1], ALU.max))
            link(dve.tensor_tensor(mid[:, 0:NG], bq[:, :, 0], bq[:, :, 1], ALU.min))
            link(dve.tensor_tensor(mid[:, NG:2 * NG], sq_[:, :, 0], sq_[:, :, 1], ALU.max))
            link(dve.tensor_tensor(mid[:, 0:NG], mid[:, 0:NG], mid[:, NG:2 * NG], ALU.max))
            link(dve.tensor_tensor(gscore[:], gscore[:], mid[:, 0:NG], ALU.add))
            gs = gscore[:].rearrange("p (s n) -> p s n", n=GROUPS)
            other = gs.unsqueeze(2).to_broadcast([P, NSUBS, GROUPS, GROUPS])
            own = gs.unsqueeze(3).to_broadcast([P, NSUBS, GROUPS, GROUPS])
            w4 = work[:].rearrange("p (s a b) -> p s a b", a=GROUPS, b=GROUPS)
            v4 = work2[:].rearrange("p (s a b) -> p s a b", a=GROUPS, b=GROUPS)
            link(dve.tensor_tensor(v4, other, own, ALU.is_equal))
            tie = g.lower8[:].unsqueeze(1).to_broadcast([P, NSUBS, GROUPS * GROUPS])
            v3 = work2[:].rearrange("p (s e) -> p s e", e=EXPERTS)
            link(dve.tensor_tensor(v3, v3, tie, ALU.mult))
            link(dve.tensor_tensor(w4, other, own, ALU.is_gt))
            link(dve.tensor_tensor(work[:], work[:], work2[:], ALU.add))
            link(dve.tensor_reduce(rank[:], work[:].rearrange("p (n b) -> p n b", b=GROUPS), AX.X, ALU.add))
            link(dve.tensor_scalar(rank[:], rank[:], TOP_GROUPS - 0.5, None, ALU.is_lt))
            cg = choice[:].rearrange("p (n e) -> p n e", e=GSIZE)
            link(dve.tensor_tensor(cg, cg, rank[:].unsqueeze(2).to_broadcast([P, NG, GSIZE]), ALU.mult))
            for k in range(NSUBS):
                i = dve.max(top8[:, k, :], choice[:, k * EXPERTS:(k + 1) * EXPERTS])
            link(i)
            for k in range(NSUBS):
                e = slice(k * EXPERTS, (k + 1) * EXPERTS)
                i = dve.match_replace(work[:, e], top8[:, k, :], choice[:, e], NEG)
            link(i)
            link(dve.tensor_scalar(work[:], work[:], NEG / 2, None, ALU.is_lt))
            link(dve.tensor_tensor(work[:], work[:], scores[:], ALU.mult))
            w3 = work[:].rearrange("p (s e) -> p s e", e=EXPERTS)
            link(dve.tensor_reduce(total[:], w3, AX.X, ALU.add))
            link(dve.tensor_scalar(total[:], total[:], 1e-20, None, ALU.add))
            link(dve.reciprocal(total[:], total[:]))
            link(dve.tensor_tensor(w3, w3, total[:].unsqueeze(2).to_broadcast([P, NSUBS, EXPERTS]), ALU.mult))
            link(dve.tensor_scalar(work[:], work[:], 2.5, None, ALU.mult))
            link(dve.tensor_copy(halves[:, :, 0:EXPERTS], w3))
            link(dve.tensor_tensor(v3, w3, halves[:, :, 0:EXPERTS], ALU.subtract))
            dve.tensor_scalar(halves[:, :, EXPERTS:2 * EXPERTS], v3, LOSCALE, None, ALU.mult).then_inc(halves_ready, 1)

        @block.tensor
        def _(pe):
            pe.wait_ge(halves_ready, 1)
            pe.wait_ge(scored, 4)
            for k in range(NSUBS):
                m = pe.transpose(g.bank[(k // 8) % 4].bitcast(F16)[:, (k % 8) * P:(k % 8 + 1) * P],
                                 halves[:, k, :], g.ident16[:])
                if k % 8 == 7:
                    m.then_inc(turned, 1)

        @block.gpsimd
        def _(pool):
            pool.memset(g.selector[0:EXPERTS, :], 1.0).then_inc(sel_zero, 1)
            pool.memset(g.selector[EXPERTS:P, :], 1.0 / LOSCALE).then_inc(sel_zero, 1)
            pool.wait_ge(sel_zero, 2)
            for h in range(2):
                s = g.selector[h * EXPERTS:(h + 1) * EXPERTS, :]
                pool.affine_select(out=s, in_=s, compare_op=ALU.is_ge, fill=0.0, base=0,
                                   pattern=[[1, ROUTED]], channel_multiplier=-INNER).then_inc(sel_zero, 1)
                pool.wait_ge(sel_zero, 3 + 2 * h)
                pool.affine_select(out=s, in_=s, compare_op=ALU.is_ge, fill=0.0, base=INNER - 1,
                                   pattern=[[-1, ROUTED]], channel_multiplier=INNER).then_inc(sel_zero, 1)
            pool.wait_ge(sel_zero, 6)


def experts(nc, g, tag, out_dram):
    with ExitStack() as ctx:
        def sb(n, s, d=F32): return ctx.enter_context(nc.sbuf_tensor(f"{tag}_{n}", s, d))
        def sem(n): return g.ctx.enter_context(nc.semaphore(f"{tag}_{n}"))
        xh, xl = sb("xh", [P, 2, TILE], F32R), sb("xl", [P, 2, TILE], F32R)
        act_buf = [sb(f"h{k}", [P, TILE]) for k in range(3)]
        hh = [sb(f"hh{k}", [P, TILE], F32R) for k in range(3)]
        hl = [sb(f"hl{k}", [P, TILE], F32R) for k in range(3)]
        ps_gate, ps_up, ps_w, ps_out = ([g.bank[2 * k], g.bank[2 * k + 1]] for k in range(4))
        x_loaded = [sem(f"x_loaded{u}") for u in range(2)]
        gate_up, w_ready, silu_done, t_ready, h_ready, hi_ready, lo_ready, down_done, added, stored = (
            sem(n) for n in ("gate_up", "w_ready", "silu_done", "t_ready", "h_ready", "hi_ready", "lo_ready",
                             "down_done", "added", "stored"))
        C = NCHUNKS
        block = ctx.enter_context(nc.Block())

        @block.sync
        def _(sp):
            def load(n, u):
                at = bass.ds(n * TILE, TILE)
                sp.dma_start(xh[:, u, :].bitcast(F32), g.xn_hi_dram[:, at]).then_inc(x_loaded[u], 16)
                sp.dma_start(xl[:, u, :].bitcast(F32), g.xn_lo_dram[:, at]).then_inc(x_loaded[u], 16)

            def store(n):
                if out_dram is not None:
                    sp.wait_ge(added, 1 + n + 1)
                    at = bass.ds(n * TILE, TILE)
                    sp.dma_start(out_dram[:, at], g.x_res[:, at]).then_inc(stored, 16)

            for u in range(2):
                load(u, u)
            with sp.Fori(0, NTILES // 2 - 1) as i:
                for u in range(2):
                    sp.wait_ge(gate_up, 1 + (2 * i + u + 1) * C)
                    load(2 * i + u + 2, u)
                    store(2 * i + u)
            for u in range(2):
                store(NTILES - 2 + u)
            if out_dram is not None:
                sp.wait_ge(stored, 16 * NTILES)

        @block.tensor
        def _(pe):
            pe.sem_inc(down_done, 1)
            pe.sem_inc(gate_up, 1)
            def product(out, wh, wl, rh, rl, start, stop):
                pe.matmul(out, wh, rh, start=start, stop=False)
                pe.matmul(out, wh, rl, start=False, stop=False)
                return pe.matmul(out, wl, rh, start=False, stop=stop)

            with pe.Fori(0, NTILES // 2) as i:
                for u in range(2):
                    base = (2 * i + u) * C
                    pe.wait_ge(x_loaded[u], 32 * i + 32)
                    for c in range(C + 2):
                        if c < C:
                            r0, rows = chunk_rows(c)
                            pe.wait_ge(silu_done, 1 + base + max(c - 1, 0))
                            product(ps_gate[c % 2][0:rows, :], g.wg_hi[:, r0:r0 + rows], g.wg_lo[:, r0:r0 + rows],
                                    xh[:, u, :], xl[:, u, :], True, True)
                            pe.wait_ge(h_ready, 1 + base + max(c - 1, 0))
                            product(ps_up[c % 2][0:rows, :], g.wu_hi[:, r0:r0 + rows], g.wu_lo[:, r0:r0 + rows],
                                    xh[:, u, :], xl[:, u, :], True, True).then_inc(gate_up, 1)
                            if c < RCHUNKS:
                                pe.matmul(ps_w[c % 2], g.selector[:, r0:r0 + P],
                                          g.wT[:, bass.ds((2 * i + u) * TILE, TILE)],
                                          start=True, stop=True).then_inc(w_ready, 1)
                        if c >= 2:
                            d = c - 2
                            rows = chunk_rows(d)[1]
                            pe.wait_ge(lo_ready, 1 + base + d + 1)
                            if d == 0:
                                pe.wait_ge(added, 1 + 2 * i)
                            product(ps_out[u], g.wd_hi[0:rows, d, :], g.wd_lo[0:rows, d, :],
                                    hh[d % 3][0:rows, :], hl[d % 3][0:rows, :], d == 0, d == C - 1).then_inc(down_done, 1)

        @block.scalar
        def _(act):
            act.sem_inc(silu_done, 1)
            with act.Fori(0, NTILES // 2) as i:
                for u in range(2):
                    base = (2 * i + u) * C
                    for c in range(C + 1):
                        if c < C:
                            rows = chunk_rows(c)[1]
                            act.wait_ge(gate_up, 1 + base + c + 1)
                            act.wait_ge(lo_ready, 1 + base + max(c - 2, 0))
                            act.activation(act_buf[c % 3][0:rows, :], ps_gate[c % 2][0:rows, :], ACT.Silu).then_inc(silu_done, 1)
                        if c >= 1:
                            d = c - 1
                            rows = chunk_rows(d)[1]
                            act.wait_ge(h_ready, 1 + base + d + 1)
                            act.wait_ge(down_done, 1 + base + max(d - 2, 0))
                            act.activation(hh[d % 3][0:rows, :], act_buf[d % 3][0:rows, :], ACT.Copy).then_inc(hi_ready, 1)

        @block.vector
        def _(dve):
            dve.sem_inc(h_ready, 1)
            dve.sem_inc(lo_ready, 1)
            dve.sem_inc(added, 1)
            with dve.Fori(0, NTILES // 2) as i:
                for u in range(2):
                    base = (2 * i + u) * C
                    tbase = (2 * i + u) * RCHUNKS
                    for c in range(C + 1):
                        if c < C:
                            rows = chunk_rows(c)[1]
                            h = act_buf[c % 3][0:rows, :]
                            dve.wait_ge(silu_done, 1 + base + c + 1)
                            t = dve.tensor_tensor(h, ps_up[c % 2][0:rows, :], h, ALU.mult)
                            t.then_inc(t_ready if c < RCHUNKS else h_ready, 1)
                        if c >= 1:
                            d = c - 1
                            rows = chunk_rows(d)[1]
                            dve.wait_ge(hi_ready, base + d + 1)
                            dve.wait_ge(down_done, 1 + base + max(d - 2, 0))
                            dve.tensor_tensor(hl[d % 3][0:rows, :], act_buf[d % 3][0:rows, :],
                                              hh[d % 3][0:rows, :].bitcast(F32), ALU.subtract).then_inc(lo_ready, 1)
                        if c < RCHUNKS:
                            dve.wait_ge(t_ready, tbase + c + 1)
                            dve.wait_ge(w_ready, tbase + c + 1)
                            dve.tensor_tensor(h, ps_w[c % 2], h, ALU.mult).then_inc(h_ready, 1)
                    dve.wait_ge(down_done, 1 + base + C)
                    x = g.x_res[:, bass.ds((2 * i + u) * TILE, TILE)]
                    dve.tensor_tensor(x, ps_out[u], x, ALU.add).then_inc(added, 1)


def flow_attention(nc, g, tag):
    with ExitStack() as ctx:
        def sb(n, s, d=F32): return ctx.enter_context(nc.sbuf_tensor(f"{tag}_{n}", s, d))
        def sem(n): return g.ctx.enter_context(nc.semaphore(f"{tag}_{n}"))
        xa = sb("xa", [P, TILE])
        qk = sb("qk", [P, 4, 2 * D])
        qke = sb("qke", [P, 4, 2 * D])
        dots = sb("dots", [P, 8 * D])
        flow = sb("flow", [P, 4, 2 * D])
        v = sb("v", [P, 4, D])
        qs = sb("qs", [P, 4, D])
        kv = sb("kv", [P, 4, HEADS * HD * HD])
        o = sb("o", [P, 4, D])
        oT = sb("oT", [P, TILE])
        inv = sb("inv", [P, 4, 2 * HEADS])
        invn = sb("invn", [P, 4, 2 * HEADS])
        cons = sb("cons", [P, 4, 2 * HEADS])
        cs = sb("cs", [P, 4, HEADS])
        alloc = sb("alloc", [P, 4, HEADS])
        comp = sb("comp", [P, 4, HEADS])
        ps_qk = g.psum[:, 0:1024]
        ps_cum = g.psum[:, 1024:2048]
        ps_kv = [g.psum[:, 2048:3072], g.psum[:, 0:1024]]
        ps_v, ps_oT = g.bank[6], g.bank[6]
        ps_cs, ps_proj = g.bank[7][:, 0:4 * HEADS], g.bank[7]
        (x_loaded, qkv_ready, qk_ready, v_copied, cum_ready, dots_ready, flow_ready, fcum_ready, cons_ready, cs_ready,
         alloc_ready, ccum_ready, vs_ready, qs_ready, kv_ready, kvcum_ready, mixed, o_ready, oT_ready, oT_copied,
         proj_ready, added, chain) = (sem(n) for n in (
             "x_loaded", "qkv_ready", "qk_ready", "v_copied", "cum_ready", "dots_ready", "flow_ready", "fcum_ready",
             "cons_ready", "cs_ready", "alloc_ready", "ccum_ready", "vs_ready", "qs_ready", "kv_ready", "kvcum_ready",
             "mixed", "o_ready", "oT_ready", "oT_copied", "proj_ready", "added", "chain"))
        NLINKS = 9
        block = ctx.enter_context(nc.Block())

        def cols(s):
            t, b = s // 2, s % 2
            return slice(b * SEQ + t * P, b * SEQ + (t + 1) * P)

        @block.sync
        def _(sp):
            with sp.Fori(0, NTILES) as i:
                sp.wait_ge(qkv_ready, 1 + i)
                sp.dma_start(xa[:], g.xn_dram[:, bass.ds(i * TILE, TILE)]).then_inc(x_loaded, 16)

        @block.tensor
        def _(pe):
            pe.sem_inc(qkv_ready, 1)
            def running(out, src):
                pe.matmul(out[0], g.tri[:], src[0], start=True, stop=True)
                pe.matmul(out[1], g.tri[:], src[1], start=True, stop=False)
                return pe.matmul(out[1], g.ones[:], src[0], start=False, stop=True)

            with pe.Fori(0, NTILES) as i:
                pe.wait_ge(x_loaded, 16 * i + 16)
                for s in range(4):
                    x = xa[:, cols(s)]
                    for out, w0, w1 in ((ps_qk[:, s * 256:(s + 1) * 256], 0, 256), (ps_v[:, s * P:(s + 1) * P], 256, 384)):
                        pe.matmul(out, x, g.wqkv_a[:, w0:w1], start=True, stop=False)
                        m = pe.matmul(out, g.ones[0:1, :], g.bqkv_a[:, w0:w1], start=False, stop=True)
                m.then_inc(qkv_ready, 1)
                pe.wait_ge(qk_ready, i + 1)
                halves = [qk[:, 2 * t:2 * t + 2, :] for t in range(2)]
                running([ps_cum[:, 0:512], ps_cum[:, 512:1024]], halves).then_inc(cum_ready, 1)
                pe.wait_ge(flow_ready, i + 1)
                halves = [flow[:, 2 * t:2 * t + 2, :] for t in range(2)]
                running([ps_cum[:, 0:512], ps_cum[:, 512:1024]], halves).then_inc(fcum_ready, 1)
                pe.wait_ge(cs_ready, i + 1)
                pe.wait_ge(added, 1 + i)
                running([ps_cs[:, 0:32], ps_cs[:, 32:64]], [cs[:, 2 * t:2 * t + 2, :] for t in range(2)]).then_inc(ccum_ready, 1)
                for s in range(4):
                    t, b = s // 2, s % 2
                    pe.wait_ge(kv_ready, 4 * i + s + 1)
                    if s >= 2:
                        pe.wait_ge(mixed, 4 * i + s - 1)
                    for c in range(2):
                        at = slice(c * 512, (c + 1) * 512)
                        out = ps_kv[s % 2][:, at]
                        m = pe.matmul(out, g.tri[:], kv[:, s, at], start=True, stop=(t == 0))
                        if t == 1:
                            m = pe.matmul(out, g.ones[:], kv[:, b, at], start=False, stop=True)
                    m.then_inc(kvcum_ready, 1)
                pe.wait_ge(o_ready, 4 * i + 4)
                pe.wait_ge(v_copied, i + 1)
                for s in range(4):
                    m = pe.transpose(ps_oT[:, cols(s)], o[:, s, :], g.ident[:])
                m.then_inc(oT_ready, 1)
                pe.wait_ge(oT_copied, i + 1)
                pe.matmul(ps_proj, g.wo_a[:], oT[:], start=True, stop=True).then_inc(proj_ready, 1)

        @block.scalar
        def _(act):
            with act.Fori(0, NTILES) as i:
                act.wait_ge(qkv_ready, 1 + i + 1)
                act.activation(qk[:].rearrange("p s d -> p (s d)"), ps_qk, ACT.Sigmoid).then_inc(qk_ready, 1)
                act.activation(v[:].rearrange("p s d -> p (s d)"), ps_v, ACT.Copy).then_inc(v_copied, 1)
                act.wait_ge(cons_ready, i + 1)
                act.activation(alloc[:], cons[:, :, HEADS:2 * HEADS], ACT.Sigmoid).then_inc(alloc_ready, 1)
                act.activation(cs[:], cons[:, :, 0:HEADS], ACT.Exp).then_inc(cs_ready, 1)
                act.wait_ge(oT_ready, i + 1)
                act.activation(oT[:], ps_oT, ACT.Copy).then_inc(oT_copied, 1)

        @block.vector
        def _(dve):
            dve.sem_inc(added, 1)
            with dve.Fori(0, NTILES) as i:
                steps = [0]

                def link(ins):
                    steps[0] += 1
                    ins.then_inc(chain, 1)
                    dve.wait_ge(chain, i * NLINKS + steps[0])

                def by_head(ap):
                    return ap.rearrange("p (n d) -> p n d", d=HD)

                def over_head(small):
                    return small.unsqueeze(3).to_broadcast([P, 4, HEADS, HD])

                def heads(ap):
                    return ap.rearrange("p s (h d) -> p s h d", d=HD)

                dve.wait_ge(qk_ready, i + 1)
                dve.tensor_scalar(qke[:, :, 0:D], qk[:, :, D:2 * D], FLOW_EPS, None, ALU.add)
                link(dve.tensor_scalar(qke[:, :, D:2 * D], qk[:, :, 0:D], FLOW_EPS, None, ALU.add))
                dve.wait_ge(cum_ready, i + 1)
                dve.scalar_tensor_tensor(dots[:], ps_cum, FLOW_EPS, qke[:].rearrange("p s d -> p (s d)"),
                                         ALU.add, ALU.mult).then_inc(dots_ready, 1)
                dve.wait_ge(dots_ready, 2 * i + 1)
                flat = inv[:].rearrange("p s h -> p (s h)")
                link(dve.tensor_reduce(flat, by_head(dots[:]), AX.X, ALU.add))
                link(dve.reciprocal(flat, flat))
                link(dve.tensor_tensor(invn[:], inv[:], g.normal[:], ALU.mult))
                dve.tensor_tensor(heads(flow[:, :, 0:D]), heads(qk[:, :, 0:D]), over_head(invn[:, :, HEADS:2 * HEADS]), ALU.mult)
                dve.tensor_tensor(heads(flow[:, :, D:2 * D]), heads(qk[:, :, D:2 * D]), over_head(invn[:, :, 0:HEADS]),
                                  ALU.mult).then_inc(flow_ready, 1)
                dve.wait_ge(fcum_ready, i + 1)
                dve.scalar_tensor_tensor(dots[:], ps_cum, FLOW_EPS, qke[:].rearrange("p s d -> p (s d)"),
                                         ALU.add, ALU.mult).then_inc(dots_ready, 1)
                dve.wait_ge(dots_ready, 2 * i + 2)
                link(dve.tensor_reduce(cons[:].rearrange("p s h -> p (s h)"), by_head(dots[:]), AX.X, ALU.add))
                dve.tensor_tensor(cons[:], cons[:], g.inv_normal[:], ALU.mult).then_inc(cons_ready, 1)
                dve.wait_ge(alloc_ready, i + 1)
                link(dve.tensor_tensor(alloc[:], alloc[:], inv[:, :, HEADS:2 * HEADS], ALU.mult))
                dve.tensor_tensor(heads(qs[:]), heads(qk[:, :, 0:D]), over_head(alloc[:]), ALU.mult).then_inc(qs_ready, 1)
                dve.wait_ge(ccum_ready, i + 1)
                dve.wait_ge(cs_ready, i + 1)
                flat_comp = comp[:].rearrange("p s h -> p (s h)")
                link(dve.reciprocal(flat_comp, ps_cs))
                link(dve.tensor_tensor(flat_comp, flat_comp, cs[:].rearrange("p s h -> p (s h)"), ALU.mult))
                link(dve.tensor_tensor(comp[:], comp[:], g.normal[:, :, 0:HEADS], ALU.mult))
                dve.wait_ge(v_copied, i + 1)
                dve.tensor_tensor(heads(v[:]), heads(v[:]), over_head(comp[:]), ALU.mult).then_inc(vs_ready, 1)
                dve.wait_ge(qs_ready, i + 1)
                for s in range(4):
                    dve.wait_ge(kvcum_ready, 4 * i + s + 1)
                    q4 = qs[:, s, :].rearrange("p (h d) -> p h d", d=HD).unsqueeze(2).to_broadcast([P, HEADS, HD, HD])
                    dve.tensor_tensor(dots[:].rearrange("p (h m d) -> p h m d", m=HD, d=HD),
                                      ps_kv[s % 2].rearrange("p (h m d) -> p h m d", m=HD, d=HD), q4, ALU.mult).then_inc(mixed, 1)
                    dve.wait_ge(mixed, 4 * i + s + 1)
                    dve.tensor_reduce(o[:, s, :], by_head(dots[:]), AX.X, ALU.add).then_inc(o_ready, 1)
                    dve.wait_ge(o_ready, 4 * i + s + 1)
                dve.wait_ge(proj_ready, i + 1)
                x = g.x_res[:, bass.ds(i * TILE, TILE)]
                dve.scalar_tensor_tensor(x, ps_proj, g.bo_a[:, 0:1], x, ALU.add, ALU.add).then_inc(added, 1)
                assert steps[0] == NLINKS, steps

        @block.gpsimd
        def _(pool):
            with pool.Fori(0, NTILES) as i:
                for s in range(4):
                    if s == 0:
                        pool.wait_ge(vs_ready, i + 1)
                    v4 = v[:, s, :].rearrange("p (h m) -> p h m", m=HD).unsqueeze(3).to_broadcast([P, HEADS, HD, HD])
                    k4 = qk[:, s, D:2 * D].rearrange("p (h d) -> p h d", d=HD).unsqueeze(2).to_broadcast([P, HEADS, HD, HD])
                    pool.tensor_tensor(kv[:, s, :].rearrange("p (h m d) -> p h m d", m=HD, d=HD), v4, k4, ALU.mult).then_inc(kv_ready, 1)


def softmax_attention(nc, g, tag):
    with ExitStack() as ctx:
        def sb(n, s, d=F32): return ctx.enter_context(nc.sbuf_tensor(f"{tag}_{n}", s, d))
        def sem(n): return g.ctx.enter_context(nc.semaphore(f"{tag}_{n}"))
        xa = sb("xa", [P, TILE])
        q_st = sb("q_st", [P, QUADS, TILE], F32R)
        k_st = sb("k_st", [P, QUADS, TILE], F32R)
        plain = sb("plain", [P, 2, TILE])
        signed = sb("signed", [P, 2, TILE], F32R)
        vv = sb("vv", [P, 4, HEADS, HD + 1])
        negmax = sb("negmax", [P, 2, HEADS])
        maxrows = sb("maxrows", [P, 2, HEADS, 32])
        prob = sb("prob", [P, 2, 1536])
        o = sb("o", [P, 4, D])
        inv = sb("inv", [P, 2, HEADS])
        oT = sb("oT", [P, TILE])
        ring = [g.psum[:, 0:1536], g.psum[:, 1536:3072]]
        (x_loaded, st_raw, st_plain, st_signed, st_ready, v_raw, v_ready, s_ready, m_ready, mrow_ready, mT_ready,
         q_ready, sT_ready, p_ready, av_ready, o_ready, oT_ready, oT_copied, proj_ready, added, chain) = (
             sem(n) for n in ("x_loaded", "st_raw", "st_plain", "st_signed", "st_ready", "v_raw", "v_ready", "s_ready",
                              "m_ready", "mrow_ready", "mT_ready", "q_ready", "sT_ready", "p_ready", "av_ready",
                              "o_ready", "oT_ready", "oT_copied", "proj_ready", "added", "chain"))
        cleared = sem("cleared")
        NST = 2 * QUADS
        NLINKS = 4
        block = ctx.enter_context(nc.Block())

        def sub(b, t):
            return slice(b * SEQ + t * P, b * SEQ + (t + 1) * P)

        @block.sync
        def _(sp):
            with sp.Fori(0, NTILES) as i:
                sp.wait_ge(v_raw, 1 + i)
                sp.dma_start(xa[:], g.xn_dram[:, bass.ds(i * TILE, TILE)]).then_inc(x_loaded, 16)

        @block.gpsimd
        def _(pool):
            pool.memset(maxrows[:], 0.0).then_inc(cleared, 1)
            pool.memset(vv[:], 1.0).then_inc(cleared, 1)

        @block.tensor
        def _(pe):
            pe.sem_inc(v_raw, 1)
            with pe.Fori(0, NTILES) as i:
                pe.wait_ge(x_loaded, 16 * i + 16)
                for n in range(NST):
                    if n >= 2:
                        pe.wait_ge(st_plain, i * NST + n - 1)
                    w = g.wq_b if n < QUADS else g.wk_b
                    pe.matmul(ring[n % 2][:, 0:512], w[:, n % QUADS, :], xa[:], start=True, stop=True).then_inc(st_raw, 1)
                pe.wait_ge(added, 1 + i)
                for s in range(4):
                    at = g.bank[7][:, s * P:(s + 1) * P]
                    pe.matmul(at, xa[:, s * P:(s + 1) * P], g.wv_b[:], start=True, stop=False)
                    m = pe.matmul(at, g.ones[0:1, :], g.bv_b[:], start=False, stop=True)
                m.then_inc(v_raw, 1)
                for b in range(2):
                    pe.wait_ge(st_ready, NST * i + NST)
                    for q in range(QUADS):
                        unit = (2 * i + b) * QUADS + q
                        r = ring[q % 2]
                        if b == 0 and q < 2:
                            pe.wait_ge(st_plain, NST * i + NST)
                        elif q < 2:
                            pe.wait_ge(p_ready, (2 * i) * 2 * QUADS + 2 * (q + 3))
                        else:
                            pe.wait_ge(m_ready, unit - 1)
                        pe.matmul(r[:, 0:512], g.ident_b[:], g.mask_key[:, 0:512], start=True, stop=False)
                        pe.matmul(r[:, 512:1024], g.ident_b[:], g.mask_key[:, 512:1024], start=True, stop=False)
                        pe.matmul(r[:, 1024:1536], g.ident_b[:], g.mask_key[:, 512:1024], start=True, stop=False)
                        rows = slice(32 * q, 32 * q + 32)
                        for h in range(QUADS):
                            qa = q_st[rows, h, :]
                            ka = k_st[rows, h, :]
                            pe.matmul(r[:, h * P:(h + 1) * P], qa[:, sub(b, 0)], ka[:, sub(b, 0)], start=False, stop=(h == 3))
                            m = pe.matmul(r[:, 512 + h * 256:768 + h * 256], qa[:, sub(b, 1)], ka[:, b * SEQ:(b + 1) * SEQ],
                                          start=False, stop=(h % 2 == 1))
                        m.then_inc(s_ready, 1)
                    pe.wait_ge(mrow_ready, 2 * i + b + 1)
                    pe.wait_ge(v_ready, i + 1)
                    if b == 1:
                        pe.wait_ge(o_ready, 2 * i + 1)
                    for t in range(2):
                        dst = g.bank[6 + t]
                        for q in range(QUADS):
                            m = pe.transpose(dst[:, q * P:(q + 1) * P],
                                             maxrows[:, t, 4 * q:4 * q + 4, :].rearrange("p h r -> p (h r)"), g.ident[:])
                    m.then_inc(mT_ready, 1)
                    pe.wait_ge(q_ready, 2 * i + b + 1)
                    for q in range(QUADS + 1):
                        if q < QUADS:
                            unit = (2 * i + b) * QUADS + q
                            r = ring[q % 2]
                            if q < 2:
                                pe.wait_ge(m_ready, (2 * i + b) * QUADS + q + 3)
                            else:
                                pe.wait_ge(p_ready, 2 * unit - 2)
                            pe.matmul(r[:, 0:512], g.ident_b[:], g.mask_query[:, 0:512], start=True, stop=False)
                            pe.matmul(r[:, 512:1024], g.ident_b[:], g.mask_query[:, 0:512], start=True, stop=False)
                            pe.matmul(r[:, 1024:1536], g.ident_b[:], g.mask_query[:, 512:1024], start=True, stop=False)
                            rows = slice(32 * q, 32 * q + 32)
                            for h in range(QUADS):
                                qa = q_st[rows, h, :]
                                ka = k_st[rows, h, :]
                                pe.matmul(r[:, h * 256:(h + 1) * 256], ka[:, sub(b, 0)], qa[:, b * SEQ:(b + 1) * SEQ],
                                          start=False, stop=(h % 2 == 1))
                                m = pe.matmul(r[:, 1024 + h * P:1024 + (h + 1) * P], ka[:, sub(b, 1)], qa[:, sub(b, 1)],
                                              start=False, stop=(h == 3))
                            m.then_inc(sT_ready, 1)
                        if q >= 1:
                            unit = (2 * i + b) * QUADS + q - 1
                            pe.wait_ge(p_ready, 2 * unit + 2)
                            for h in range(4):
                                head = 4 * h + q - 1
                                pr = prob[:, (q - 1) % 2, :]
                                o0 = g.bank[6][:, head * 9:head * 9 + 9]
                                o1 = g.bank[6][:, (HEADS + head) * 9:(HEADS + head) * 9 + 9]
                                pe.matmul(o0, pr[:, h * 256:h * 256 + P], vv[:, 2 * b, head, :], start=True, stop=True)
                                pe.matmul(o1, pr[:, h * 256 + P:h * 256 + 256], vv[:, 2 * b, head, :], start=True, stop=False)
                                m = pe.matmul(o1, pr[:, 1024 + h * P:1024 + (h + 1) * P], vv[:, 2 * b + 1, head, :],
                                              start=False, stop=True)
                            m.then_inc(av_ready, 1)
                pe.wait_ge(o_ready, 2 * i + 2)
                for s in range(4):
                    m = pe.transpose(g.bank[6][:, s * P:(s + 1) * P], o[:, s, :], g.ident[:])
                m.then_inc(oT_ready, 1)
                pe.wait_ge(oT_copied, i + 1)
                pe.matmul(g.bank[7], g.wo_b[:], oT[:], start=True, stop=True).then_inc(proj_ready, 1)

        @block.scalar
        def _(act):
            with act.Fori(0, NTILES) as i:
                for n in range(NST):
                    act.wait_ge(st_raw, i * NST + n + 1)
                    if n >= 2:
                        act.wait_ge(st_ready, i * NST + n - 1)
                    bias = (g.bq_b if n < QUADS else g.bk_b)[:, n % QUADS:n % QUADS + 1]
                    act.activation(plain[:, n % 2, :], ring[n % 2][:, 0:512], ACT.Identity, bias=bias).then_inc(st_plain, 1)
                    act.wait_ge(st_plain, i * NST + n + 1)
                    sign = g.split[:, 0:1] if n < QUADS else g.split[:, 2:3]
                    act.activation(signed[:, n % 2, :], plain[:, n % 2, :], ACT.Copy, scale=sign).then_inc(st_signed, 1)
                act.wait_ge(v_raw, 1 + i + 1)
                act.wait_ge(cleared, 2)
                act.activation(vv[:, :, :, 0:HD], g.bank[7].rearrange("p (s h d) -> p s h d", s=4, d=HD), ACT.Copy).then_inc(v_ready, 1)
                for b in range(2):
                    for q in range(QUADS):
                        unit = (2 * i + b) * QUADS + q
                        act.wait_ge(sT_ready, unit + 1)
                        if q >= 2:
                            act.wait_ge(av_ready, unit - 1)
                        act.activation(prob[:, q % 2, 0:1024], ring[q % 2][:, 0:1024], ACT.Exp, scale=SCALE).then_inc(p_ready, 1)
                        act.activation(prob[:, q % 2, 1024:1536], ring[q % 2][:, 1024:1536], ACT.Exp, scale=SCALE).then_inc(p_ready, 1)
                act.wait_ge(oT_ready, i + 1)
                act.activation(oT[:], g.bank[6], ACT.Copy).then_inc(oT_copied, 1)

        @block.vector
        def _(dve):
            dve.sem_inc(added, 1)
            with dve.Fori(0, NTILES) as i:
                steps = [0]

                def link(ins):
                    steps[0] += 1
                    ins.then_inc(chain, 1)
                    dve.wait_ge(chain, i * NLINKS + steps[0])

                for n in range(NST):
                    dve.wait_ge(st_signed, i * NST + n + 1)
                    low = g.split[:, 1:2] if n < QUADS else g.split[:, 3:4]
                    dst = (q_st if n < QUADS else k_st)[:, n % QUADS, :]
                    dve.scalar_tensor_tensor(dst, plain[:, n % 2, :], low, signed[:, n % 2, :].bitcast(F32),
                                             ALU.mult, ALU.add).then_inc(st_ready, 1)
                for b in range(2):
                    for q in range(QUADS):
                        r = ring[q % 2]
                        dve.wait_ge(s_ready, (2 * i + b) * QUADS + q + 1)
                        dve.tensor_reduce(negmax[:, 0, q:HEADS:4], r[:, 0:512].rearrange("p (h k) -> p h k", k=P),
                                          AX.X, ALU.max, negate=True)
                        dve.tensor_reduce(negmax[:, 1, q:HEADS:4], r[:, 512:1536].rearrange("p (h k) -> p h k", k=SEQ),
                                          AX.X, ALU.max, negate=True).then_inc(m_ready, 1)
                    dve.wait_ge(m_ready, (2 * i + b + 1) * QUADS)
                    dve.wait_ge(cleared, 2)
                    link(dve.tensor_copy(maxrows[:, :, :, 24].bitcast(F32R), negmax[:]))
                    dve.tensor_tensor(maxrows[:, :, :, 25], negmax[:], maxrows[:, :, :, 24], ALU.subtract).then_inc(mrow_ready, 1)
                    dve.wait_ge(mT_ready, 2 * i + b + 1)
                    for t in range(2):
                        qa = q_st[:, :, sub(b, t)]
                        m = dve.tensor_tensor(qa, g.bank[6 + t].rearrange("p (q k) -> p q k", k=P), qa.bitcast(F32), ALU.add)
                    m.then_inc(q_ready, 1)
                    dve.wait_ge(av_ready, (2 * i + b + 1) * QUADS)
                    av = g.bank[6][:, 0:2 * HEADS * 9].rearrange("p (t h e) -> p t h e", t=2, e=9)
                    link(dve.reciprocal(inv[:], av[:, :, :, 8]))
                    dve.tensor_tensor(o[:, 2 * b:2 * b + 2, :].rearrange("p t (h d) -> p t h d", d=HD), av[:, :, :, 0:HD],
                                      inv[:].unsqueeze(3).to_broadcast([P, 2, HEADS, HD]), ALU.mult).then_inc(o_ready, 1)
                dve.wait_ge(proj_ready, i + 1)
                x = g.x_res[:, bass.ds(i * TILE, TILE)]
                dve.scalar_tensor_tensor(x, g.bank[7], g.bo_b[:, 0:1], x, ALU.add, ALU.add).then_inc(added, 1)
                assert steps[0] == NLINKS, steps


def setup(nc, g, ins, tag, first):
    with ExitStack() as ctx:
        def sem(n): return g.ctx.enter_context(nc.semaphore(f"{tag}_{n}"))
        loaded, made, inverted = sem("loaded"), sem("made"), sem("inverted")
        iota = ctx.enter_context(nc.sbuf_tensor(f"{tag}_iota", [P, 4 * 2 * HEADS], I32))
        normal_step = []
        block = ctx.enter_context(nc.Block())

        @block.sync
        def _(sp):
            pairs = [(g.x_res[:], ins["xT"]), (g.gate_wT[:], ins["gate_wT"]),
                     (g.gate_bias[:], ins["gate_bias"].partition_broadcast(P)),
                     (g.lower8[:], ins["lower8"].partition_broadcast(P))] if first else []
            pairs += [
                     (g.wqkv_a[:], ins["wqkv_a"]), (g.bqkv_a[:], ins["bqkv_a"]), (g.wo_a[:], ins["wo_a"]),
                     (g.bo_a[:], ins["bo_a"]), (g.wq_b[:], ins["wq_b"]), (g.wk_b[:], ins["wk_b"]),
                     (g.wv_b[:], ins["wv_b"]), (g.bv_b[:], ins["bv_b"]), (g.wo_b[:], ins["wo_b"]),
                     (g.bo_b[:], ins["bo_b"]), (g.bq_b[:], ins["bq_b"]), (g.bk_b[:], ins["bk_b"]),
                     (g.split[:], ins["split"])]
            for dst, src in pairs:
                sp.dma_start(dst, src).then_inc(loaded, 16)
            sp.wait_ge(loaded, 16 * len(pairs))

        @block.gpsimd
        def _(pool):
            k = [0]

            def then(ins):
                k[0] += 1
                ins.then_inc(made, 1)
                pool.wait_ge(made, k[0])

            then(pool.memset(g.ones[:], 1.0))
            then(pool.memset(g.ones_d[:], 1.0 / D))
            then(pool.memset(g.ln_eps[:], LN_EPS))
            then(pool.memset(g.ident_f[:], 1.0))
            then(pool.affine_select(out=g.ident[:], in_=g.ident_f[:], compare_op=ALU.is_equal, fill=0.0, base=0,
                                    pattern=[[-1, P]], channel_multiplier=1))
            then(pool.affine_select(out=g.tri[:], in_=g.ident_f[:], compare_op=ALU.is_ge, fill=0.0, base=0,
                                    pattern=[[1, P]], channel_multiplier=-1))
            then(pool.tensor_copy(g.ident16[:], g.ident[:]))
            then(pool.tensor_copy(g.ident_b[:], g.ident[:]))
            then(pool.memset(g.mask_key[:], 0.0))
            then(pool.memset(g.mask_query[:], 0.0))
            first = g.mask_key[:, 0:512].rearrange("p (h k) -> p h k", k=P)
            then(pool.affine_select(out=first, in_=first, compare_op=ALU.is_ge, fill=NEG, base=0,
                                    pattern=[[0, 4], [-1, P]], channel_multiplier=1))
            second = g.mask_key[:, 512:1024].rearrange("p (h t k) -> p h t k", t=2, k=P)[:, :, 1, :]
            then(pool.affine_select(out=second, in_=second, compare_op=ALU.is_ge, fill=NEG, base=0,
                                    pattern=[[0, 2], [-1, P]], channel_multiplier=1))
            first = g.mask_query[:, 0:512].rearrange("p (h t k) -> p h t k", t=2, k=P)[:, :, 0, :]
            then(pool.affine_select(out=first, in_=first, compare_op=ALU.is_ge, fill=NEG, base=0,
                                    pattern=[[0, 2], [1, P]], channel_multiplier=-1))
            second = g.mask_query[:, 512:1024].rearrange("p (h k) -> p h k", k=P)
            then(pool.affine_select(out=second, in_=second, compare_op=ALU.is_ge, fill=NEG, base=0,
                                    pattern=[[0, 4], [1, P]], channel_multiplier=-1))
            then(pool.iota(iota[:], pattern=[[P, 2], [0, 4 * HEADS]], base=1, channel_multiplier=1))
            then(pool.tensor_copy(g.normal[:].rearrange("p s h -> p (s h)"), iota[:]))
            normal_step.append(k[0])


        @block.vector
        def _(dve):
            dve.wait_ge(made, normal_step[0])
            dve.reciprocal(g.inv_normal[:], g.normal[:]).then_inc(inverted, 1)


def split_weights(nc, g, ins, tag):
    with ExitStack() as ctx:
        def sem(n): return g.ctx.enter_context(nc.semaphore(f"{tag}_{n}"))
        W = 1024
        stage = ctx.enter_context(nc.sbuf_tensor(f"{tag}_stage", [P, 4, W], F32))
        jobs = []
        for name, hi, lo in (("wg", g.wg_hi, g.wg_lo), ("wu", g.wu_hi, g.wu_lo)):
            for a in range(0, ROUTED + SHARED, W):
                n = min(W, ROUTED + SHARED - a)
                jobs.append((P, n, ins[name][:, a:a + n], hi[:, a:a + n], lo[:, a:a + n]))
        per = W // D
        for a in range(0, RCHUNKS, per):
            n = min(per, RCHUNKS - a)
            src = ins["wd"][a * P:(a + n) * P, :].rearrange("(c p) d -> p c d", p=P)
            jobs.append((P, n * D, src, g.wd_hi[:, a:a + n, :], g.wd_lo[:, a:a + n, :]))
        src = ins["wd"][ROUTED:, :].rearrange("(c p) d -> p c d", p=INNER)
        jobs.append((INNER, 2 * D, src, g.wd_hi[0:INNER, RCHUNKS:, :], g.wd_lo[0:INNER, RCHUNKS:, :]))
        loaded = [sem(f"loaded{k}") for k in range(4)]
        hi_ready, lo_ready = sem("hi_ready"), sem("lo_ready")
        block = ctx.enter_context(nc.Block())

        def shaped(k, rows, n, like):
            s = stage[0:rows, k % 4, 0:n]
            return s if len(like.shape) == 2 else s.rearrange("p (c d) -> p c d", d=D)

        @block.sync
        def _(sp):
            for k, (rows, n, src, hi, lo) in enumerate(jobs):
                if k >= 4:
                    sp.wait_ge(lo_ready, k - 3)
                sp.dma_start(shaped(k, rows, n, hi), src).then_inc(loaded[k % 4], 16)

        @block.scalar
        def _(act):
            for k, (rows, n, src, hi, lo) in enumerate(jobs):
                act.wait_ge(loaded[k % 4], 16 * (k // 4 + 1))
                act.activation(hi, shaped(k, rows, n, hi), ACT.Copy).then_inc(hi_ready, 1)

        @block.vector
        def _(dve):
            for k, (rows, n, src, hi, lo) in enumerate(jobs):
                dve.wait_ge(hi_ready, k + 1)
                dve.wait_ge(loaded[k % 4], 16 * (k // 4 + 1))
                dve.tensor_tensor(lo, shaped(k, rows, n, hi), hi.bitcast(F32), ALU.subtract).then_inc(lo_ready, 1)


def build(nc, ins, outT):
    with ExitStack() as ctx:
        g = Shared()
        g.ctx = ctx
        def sb(n, s, d=F32): return ctx.enter_context(nc.sbuf_tensor(n, s, d))
        g.psum = ctx.enter_context(nc.psum_tensor("psum", [P, 8 * 512], F32))
        g.bank = [g.psum[:, k * 512:(k + 1) * 512] for k in range(8)]
        g.x_res = sb("x_res", [P, TOKENS])
        R = ROUTED + SHARED
        g.gate_wT, g.gate_bias, g.lower8 = sb("gate_wT", [P, EXPERTS]), sb("gate_bias", [P, EXPERTS]), sb("lower8", [P, 64])
        g.wo_b, g.bo_b = sb("wo_b", [P, D]), sb("bo_b", [P, 1])
        g.ones_d, g.ident, g.ident16, g.ln_eps = sb("ones_d", [P, P]), sb("ident", [P, P]), sb("ident16", [P, P], F16), sb("ln_eps", [P, 1])
        g.xn_dram = nc.dram_tensor("xn_scratch", [P, TOKENS], F32, kind="Internal").ap()
        g.xn_hi_dram = nc.dram_tensor("xn_hi_scratch", [P, TOKENS], F32, kind="Internal").ap()
        g.xn_lo_dram = nc.dram_tensor("xn_lo_scratch", [P, TOKENS], F32, kind="Internal").ap()

        def constants(c2, tag):
            def sc(n, s, d=F32): return c2.enter_context(nc.sbuf_tensor(f"{tag}_{n}", s, d))
            g.wqkv_a, g.bqkv_a, g.wo_a, g.bo_a = sc("wqkv_a", [P, 3 * D]), sc("bqkv_a", [1, 3 * D]), sc("wo_a", [P, D]), sc("bo_a", [P, 1])
            g.wq_b, g.wk_b = sc("wq_b", [P, QUADS, P]), sc("wk_b", [P, QUADS, P])
            g.bq_b, g.bk_b, g.split = sc("bq_b", [P, QUADS]), sc("bk_b", [P, QUADS]), sc("split", [P, 4])
            g.wv_b, g.bv_b = sc("wv_b", [P, D]), sc("bv_b", [1, D])
            g.ones, g.tri, g.ident_f, g.ident_b = sc("ones", [P, P]), sc("tri", [P, P]), sc("ident_f", [P, P]), sc("ident_b", [P, P], BF16)
            g.mask_key, g.mask_query = sc("mask_key", [P, 1024], BF16), sc("mask_query", [P, 1024], BF16)
            g.normal, g.inv_normal = sc("normal", [P, 4, 2 * HEADS]), sc("inv_normal", [P, 4, 2 * HEADS])

        def weights(c2, tag):
            def sc(n, s, d=F32): return c2.enter_context(nc.sbuf_tensor(f"{tag}_{n}", s, d))
            g.wg_hi, g.wg_lo, g.wu_hi, g.wu_lo = (sc(n, [P, R], F32R) for n in ("wg_hi", "wg_lo", "wu_hi", "wu_lo"))
            g.wd_hi, g.wd_lo = (sc(n, [P, NCHUNKS, D], F32R) for n in ("wd_hi", "wd_lo"))

        def moe(tag, out_dram):
            with ExitStack() as c3:
                g.wT = c3.enter_context(nc.sbuf_tensor(f"{tag}_wT", [P, TOKENS], F16))
                g.selector = c3.enter_context(nc.sbuf_tensor(f"{tag}_selector", [P, ROUTED], F16))
                layernorm(nc, g, f"{tag}_ln", True)
                routing(nc, g, f"{tag}_route")
                weights(c3, tag)
                split_weights(nc, g, ins, f"{tag}_split")
                experts(nc, g, f"{tag}_exp", out_dram)

        with ExitStack() as keep:
            constants(keep, "flow")
            setup(nc, g, ins, "flow_setup", True)
            layernorm(nc, g, "flow_ln", False)
            flow_attention(nc, g, "flow")
        moe("moe1", None)
        with ExitStack() as keep:
            constants(keep, "attn")
            setup(nc, g, ins, "attn_setup", False)
            layernorm(nc, g, "attn_ln", False)
            softmax_attention(nc, g, "attn")
        moe("moe2", outT)


def lay_out(a):
    f = np.float32
    def cat(*x): return np.ascontiguousarray(np.concatenate(x, axis=0))
    cw, cb = np.asarray(a["L0_attn_b_c_attn_w"]), np.asarray(a["L0_attn_b_c_attn_b"])

    def stack(w, b, ones):
        ws, bs = np.zeros((D, QUADS, 4, 4, HD), f), np.zeros((QUADS, 4, 4, HD), f)
        for r in range(3):
            ws[:, :, :, r, :] = w.reshape(D, QUADS, 4, HD)
            bs[:, :, r, :] = b.reshape(QUADS, 4, HD)
        if ones:
            bs[:, :, 3, 0:2] = 1.0
        return ws.reshape(D, QUADS, P), np.ascontiguousarray(bs.reshape(QUADS, P).T)

    wq, bq = stack(cw[:, 0:D], cb[0:D], False)
    wk, bk = stack(cw[:, D:2 * D], cb[D:2 * D], True)
    split = np.zeros((4, 4, HD, 4), f)
    split[..., 0], split[..., 2] = 1.0, 1.0
    split[:, 2, :, 0], split[:, 2, :, 1] = -1.0, 1.0
    split[:, 1, :, 2], split[:, 1, :, 3] = -1.0, 1.0
    x = np.asarray(a["L0_attn_a_x"]).reshape(TOKENS, D)
    return {
        "xT": np.ascontiguousarray(x.T),
        "wqkv_a": np.ascontiguousarray(np.concatenate([a["L0_attn_a_Wq"], a["L0_attn_a_Wk"], a["L0_attn_a_Wv"]], axis=1)),
        "bqkv_a": np.concatenate([a["L0_attn_a_bq"], a["L0_attn_a_bk"], a["L0_attn_a_bv"]]).reshape(1, 3 * D),
        "wo_a": np.asarray(a["L0_attn_a_Wo"]), "bo_a": np.asarray(a["L0_attn_a_bo"]).reshape(D, 1),
        "wq_b": wq, "wk_b": wk, "bq_b": bq, "bk_b": bk, "split": split.reshape(P, 4),
        "wv_b": np.ascontiguousarray(cw[:, 2 * D:]), "bv_b": cb[2 * D:].reshape(1, D),
        "wo_b": np.asarray(a["L0_attn_b_c_proj_w"]), "bo_b": np.asarray(a["L0_attn_b_c_proj_b"]).reshape(D, 1),
        "gate_wT": np.ascontiguousarray(np.asarray(a["L0_ffn_gate_w"]).T),
        "gate_bias": np.asarray(a["L0_ffn_gate_bias"]),
        "lower8": np.tril(np.ones((8, 8), f), -1).reshape(64),
        "wg": np.ascontiguousarray(cat(np.asarray(a["L0_ffn_Wg"]).reshape(ROUTED, D), a["L0_ffn_Sg"]).T),
        "wu": np.ascontiguousarray(cat(np.asarray(a["L0_ffn_Wu"]).reshape(ROUTED, D), a["L0_ffn_Su"]).T),
        "wd": cat(np.asarray(a["L0_ffn_Wd"]).transpose(0, 2, 1).reshape(ROUTED, D), np.asarray(a["L0_ffn_Sd"]).T),
    }


def kernel(**inputs):
    import concourse.bacc as _bacc
    from concourse.bass_utils import run_bass_kernel_spmd as _run

    nc = _bacc.Bacc("TRN2", target_bir_lowering=False, num_devices=1)
    arrays, ins = {}, {}
    for name, a in lay_out(inputs).items():
        arrays[f"in_{name}_dram"] = a
        ins[name] = nc.dram_tensor(f"in_{name}_dram", a.shape, mybir.dt.from_np(a.dtype), kind="ExternalInput").ap()
    outT = nc.dram_tensor("outT_dram", (D, TOKENS), F32, kind="ExternalOutput").ap()
    build(nc, ins, outT)
    r = _run(nc, [arrays], core_ids=[0])
    return np.ascontiguousarray(r.results[0]["outT_dram"].T).reshape(BATCH, SEQ, D)
```

```python
from contextlib import ExitStack

import numpy as np

import concourse.bass as bass
from concourse import mybir

F32 = mybir.dt.float32
F32R = mybir.dt.float32r
F16 = mybir.dt.float16
BF16 = mybir.dt.bfloat16
I32 = mybir.dt.int32
ACT = mybir.ActivationFunctionType
ALU = mybir.AluOpType
AX = mybir.AxisListType

P = 128
D = 128
BATCH, SEQ = 16, 256
TOKENS = BATCH * SEQ
TILE = 512
NTILES = TOKENS // TILE
NSUB = TILE // P
HEADS, HD = 16, 8
QUADS = HEADS // 4
EXPERTS, INNER = 64, 88
GROUPS, GSIZE, TOP_GROUPS = 8, 8, 4
ROUTED = EXPERTS * INNER
SHARED = 2 * INNER
RCHUNKS = ROUTED // P
NCHUNKS = RCHUNKS + 2
SPLIT_COLS = 1024
LN_EPS = 1e-5
FLOW_EPS = 1e-6
NEG = -1.0e30
SCALE = 1.0 / float(np.sqrt(HD))
LOSCALE = 2048.0
NSUBS = TOKENS // P


class Shared:
    pass


def chunk_rows(c):
    return (c * P, P) if c < RCHUNKS else (ROUTED + (c - RCHUNKS) * INNER, INNER)


def layernorm(nc, g, tag, logits):
    with ExitStack() as ctx:
        def sb(n, s, d=F32): return ctx.enter_context(nc.sbuf_tensor(f"{tag}_{n}", s, d))
        def sem(n): return g.ctx.enter_context(nc.semaphore(f"{tag}_{n}"))
        xc = sb("xc", [P, 3, TILE])
        sq, diag, xn = (sb(n, [P, 2, TILE]) for n in ("sq", "diag", "xn"))
        sd, rstd = sb("sd", [P, 2, NSUB]), sb("rstd", [P, 2, NSUB])
        if logits:
            hi, lo = sb("hi", [P, 2, TILE], F32R), sb("lo", [P, 2, TILE], F32R)
        mean, var, spread = [g.bank[0], g.bank[1]], g.bank[2][:, 0:NSUB], g.bank[3]
        mean_ready, centred, squared, var_ready, sd_ready, inverted, diag_ready, spread_ready, normed = (
            sem(n) for n in ("mean_ready", "centred", "squared", "var_ready", "sd_ready", "inverted", "diag_ready",
                             "spread_ready", "normed"))
        if logits:
            hi_ready, lo_ready, logits_ready, sel_zero = (sem(n) for n in ("hi_ready", "lo_ready", "logits_ready",
                                                                           "sel_zero"))
        stored = [sem(f"stored{u}") for u in range(2)]
        stores = 2 if logits else 1
        block = ctx.enter_context(nc.Block())

        @block.tensor
        def _(pe):
            for n in range(NTILES + 3):
                if n < NTILES:
                    if n >= 2:
                        pe.wait_ge(centred, n - 1)
                    pe.matmul(mean[n % 2], g.ones_d[:], g.x_res[:, n * TILE:(n + 1) * TILE],
                              start=True, stop=True).then_inc(mean_ready, 1)
                if 1 <= n <= NTILES:
                    m = n - 1
                    pe.wait_ge(squared, m + 1)
                    if m >= 1:
                        pe.wait_ge(sd_ready, m)
                    for s in range(NSUB):
                        mm = pe.matmul(var[:, s:s + 1], sq[:, m % 2, s * P:(s + 1) * P], g.ones_d[:, 0:1],
                                       start=True, stop=True)
                    mm.then_inc(var_ready, 1)
                if 2 <= n <= NTILES + 1:
                    m = n - 2
                    pe.wait_ge(diag_ready, m + 1)
                    if m >= 1:
                        pe.wait_ge(normed, m)
                    pe.matmul(spread, g.ones[:], diag[:, m % 2, :], start=True, stop=True).then_inc(spread_ready, 1)
                if logits and n >= 3:
                    m = n - 3
                    pe.wait_ge(normed, m + 1)
                    for s in range(NSUB):
                        k = m * NSUB + s
                        mm = pe.matmul(g.bank[4 + k // 8][:, (k % 8) * EXPERTS:(k % 8 + 1) * EXPERTS],
                                       xn[:, m % 2, s * P:(s + 1) * P], g.gate_wT[:], start=True, stop=True)
                    mm.then_inc(logits_ready, 1)

        @block.vector
        def _(dve):
            for n in range(NTILES + 3):
                if n < NTILES:
                    dve.wait_ge(mean_ready, n + 1)
                    if n >= 3:
                        dve.wait_ge(squared, n - 2)
                        dve.wait_ge(normed, n - 2)
                    dve.tensor_tensor(xc[:, n % 3, :], g.x_res[:, n * TILE:(n + 1) * TILE], mean[n % 2],
                                      ALU.subtract).then_inc(centred, 1)
                if 1 <= n <= NTILES:
                    m = n - 1
                    dve.wait_ge(sd_ready, m + 1)
                    dve.reciprocal(rstd[:, m % 2, :], sd[:, m % 2, :]).then_inc(inverted, 1)
                    dve.wait_ge(inverted, m + 1)
                    if m >= 2:
                        dve.wait_ge(spread_ready, m - 1)
                    for s in range(NSUB):
                        i = dve.tensor_scalar(diag[:, m % 2, s * P:(s + 1) * P], g.ident[:], rstd[:, m % 2, s:s + 1],
                                              None, ALU.mult)
                    i.then_inc(diag_ready, 1)
                if 2 <= n <= NTILES + 1:
                    m = n - 2
                    dve.wait_ge(spread_ready, m + 1)
                    dve.wait_ge(centred, m + 1)
                    if m >= 2:
                        if logits:
                            dve.wait_ge(logits_ready, m - 1)
                            dve.wait_ge(hi_ready, m - 1)
                            dve.wait_ge(lo_ready, m - 1)
                        else:
                            dve.wait_ge(stored[m % 2], 16 * (m // 2))
                    dve.tensor_tensor(xn[:, m % 2, :], xc[:, m % 3, :], spread, ALU.mult).then_inc(normed, 1)
                if logits and n >= 3:
                    m = n - 3
                    dve.wait_ge(hi_ready, m + 1)
                    dve.wait_ge(normed, m + 1)
                    if m >= 2:
                        dve.wait_ge(stored[m % 2], 32 * (m // 2))
                    dve.tensor_tensor(lo[:, m % 2, :], xn[:, m % 2, :], hi[:, m % 2, :].bitcast(F32),
                                      ALU.subtract).then_inc(lo_ready, 1)

        @block.scalar
        def _(act):
            for n in range(NTILES + 2):
                if n < NTILES:
                    act.wait_ge(centred, n + 1)
                    if n >= 2:
                        act.wait_ge(var_ready, n - 1)
                    act.activation(sq[:, n % 2, :], xc[:, n % 3, :], ACT.Square).then_inc(squared, 1)
                if 1 <= n <= NTILES:
                    m = n - 1
                    act.wait_ge(var_ready, m + 1)
                    if m >= 2:
                        act.wait_ge(inverted, m - 1)
                    act.activation(sd[:, m % 2, :], var, ACT.Sqrt, bias=g.ln_eps[:, 0:1]).then_inc(sd_ready, 1)
                if logits and n >= 2:
                    m = n - 2
                    act.wait_ge(normed, m + 1)
                    if m >= 2:
                        act.wait_ge(stored[m % 2], 32 * (m // 2))
                        act.wait_ge(lo_ready, m - 1)
                    act.activation(hi[:, m % 2, :], xn[:, m % 2, :], ACT.Copy).then_inc(hi_ready, 1)

        @block.sync
        def _(sp):
            for n in range(NTILES):
                at = slice(n * TILE, (n + 1) * TILE)
                if logits:
                    sp.wait_ge(hi_ready, n + 1)
                    sp.dma_start(g.xn_hi_dram[:, at], hi[:, n % 2, :].bitcast(F32)).then_inc(stored[n % 2], 16)
                    sp.wait_ge(lo_ready, n + 1)
                    sp.dma_start(g.xn_lo_dram[:, at], lo[:, n % 2, :].bitcast(F32)).then_inc(stored[n % 2], 16)
                else:
                    sp.wait_ge(normed, n + 1)
                    sp.dma_start(g.xn_dram[:, at], xn[:, n % 2, :]).then_inc(stored[n % 2], 16)
            for u in range(2):
                sp.wait_ge(stored[u], 16 * stores * (NTILES // 2))

        @block.gpsimd
        def _(pool):
            if not logits:
                return
            pool.memset(g.selector[0:EXPERTS, :], 1.0).then_inc(sel_zero, 1)
            pool.memset(g.selector[EXPERTS:P, :], 1.0 / LOSCALE).then_inc(sel_zero, 1)
            pool.wait_ge(sel_zero, 2)
            for h in range(2):
                s = g.selector[h * EXPERTS:(h + 1) * EXPERTS, :]
                pool.affine_select(out=s, in_=s, compare_op=ALU.is_ge, fill=0.0, base=0,
                                   pattern=[[1, ROUTED]], channel_multiplier=-INNER).then_inc(sel_zero, 1)
                pool.wait_ge(sel_zero, 3 + 2 * h)
                pool.affine_select(out=s, in_=s, compare_op=ALU.is_ge, fill=0.0, base=INNER - 1,
                                   pattern=[[-1, ROUTED]], channel_multiplier=INNER).then_inc(sel_zero, 1)
            pool.wait_ge(sel_zero, 6)


def routing(nc, g, ins, tag):
    with ExitStack() as ctx:
        def sb(n, s, d=F32): return ctx.enter_context(nc.sbuf_tensor(f"{tag}_{n}", s, d))
        def sem(n): return g.ctx.enter_context(nc.semaphore(f"{tag}_{n}"))
        N = NSUBS * EXPERTS
        scores = sb("scores", [P, N])
        choice = sb("choice", [P, N])
        work = sb("work", [P, N])
        work2 = sb("work2", [P, N])
        halves = choice[:].bitcast(F16).rearrange("p (s e) -> p s e", e=2 * EXPERTS)
        NG = NSUBS * GROUPS
        big1, small1 = sb("big1", [P, NG * 4]), work2
        big2, small2 = sb("big2", [P, NG * 2]), sb("small2", [P, NG * 2])
        mid = sb("mid", [P, NG * 2])
        gscore, rank = sb("gscore", [P, NG]), sb("rank", [P, NG])
        top8 = sb("top8", [P, NSUBS, 8])
        total = sb("total", [P, NSUBS])
        scored, chain, halves_ready, turned, copied = (
            sem(n) for n in ("scored", "chain", "halves_ready", "turned", "copied"))
        stage = sb("stage", [P, 4, SPLIT_COLS])
        w_loaded = g.w_loaded = [sem(f"w_loaded{k}") for k in range(4)]
        w_hi_ready, w_lo_ready = g.w_hi_ready, g.w_lo_ready = sem("w_hi_ready"), sem("w_lo_ready")
        jobs = []
        for name, hi, lo in (("wg", g.wg_hi, g.wg_lo), ("wu", g.wu_hi, g.wu_lo)):
            for a in range(0, ROUTED + SHARED, SPLIT_COLS):
                at = slice(a, min(a + SPLIT_COLS, ROUTED + SHARED))
                jobs.append((ins[name][:, at], hi[:, at], lo[:, at]))
        g.jobs_done = len(jobs)
        block = ctx.enter_context(nc.Block())

        @block.scalar
        def _(act):
            for k in range(4):
                i = act.activation(scores[:, k * 512:(k + 1) * 512], g.bank[4 + k], ACT.Sigmoid)
                i.then_inc(scored, 1)
            for k, (src, hi, lo) in enumerate(jobs):
                act.wait_ge(w_loaded[k % 4], 16 * (k // 4 + 1))
                act.activation(hi, stage[:, k % 4, 0:src.shape[1]], ACT.Copy).then_inc(w_hi_ready, 1)
            for k in range(NSUBS // 8):
                act.wait_ge(turned, k + 1)
                act.activation(g.wT[:, k * 1024:(k + 1) * 1024], g.bank[k % 4].bitcast(F16), ACT.Copy).then_inc(copied, 1)

        @block.vector
        def _(dve):
            steps = [0]

            def link(ins):
                steps[0] += 1
                ins.then_inc(chain, 1)
                dve.wait_ge(chain, steps[0])

            dve.wait_ge(scored, 4)
            c3 = choice[:].rearrange("p (s e) -> p s e", e=EXPERTS)
            link(dve.tensor_tensor(c3, scores[:].rearrange("p (s e) -> p s e", e=EXPERTS),
                                   g.gate_bias[:].unsqueeze(1).to_broadcast([P, NSUBS, EXPERTS]), ALU.add))
            pair = choice[:].rearrange("p (n two) -> p n two", two=2)
            link(dve.tensor_tensor(big1[:], pair[:, :, 0], pair[:, :, 1], ALU.max))
            link(dve.tensor_tensor(small1[:, 0:NG * 4], pair[:, :, 0], pair[:, :, 1], ALU.min))
            bp = big1[:].rearrange("p (n two) -> p n two", two=2)
            sp_ = small1[:, 0:NG * 4].rearrange("p (n two) -> p n two", two=2)
            link(dve.tensor_tensor(big2[:], bp[:, :, 0], bp[:, :, 1], ALU.max))
            link(dve.tensor_tensor(mid[:], bp[:, :, 0], bp[:, :, 1], ALU.min))
            link(dve.tensor_tensor(small2[:], sp_[:, :, 0], sp_[:, :, 1], ALU.max))
            link(dve.tensor_tensor(small2[:], small2[:], mid[:], ALU.max))
            bq = big2[:].rearrange("p (n two) -> p n two", two=2)
            sq_ = small2[:].rearrange("p (n two) -> p n two", two=2)
            link(dve.tensor_tensor(gscore[:], bq[:, :, 0], bq[:, :, 1], ALU.max))
            link(dve.tensor_tensor(mid[:, 0:NG], bq[:, :, 0], bq[:, :, 1], ALU.min))
            link(dve.tensor_tensor(mid[:, NG:2 * NG], sq_[:, :, 0], sq_[:, :, 1], ALU.max))
            link(dve.tensor_tensor(mid[:, 0:NG], mid[:, 0:NG], mid[:, NG:2 * NG], ALU.max))
            link(dve.tensor_tensor(gscore[:], gscore[:], mid[:, 0:NG], ALU.add))
            gs = gscore[:].rearrange("p (s n) -> p s n", n=GROUPS)
            other = gs.unsqueeze(2).to_broadcast([P, NSUBS, GROUPS, GROUPS])
            own = gs.unsqueeze(3).to_broadcast([P, NSUBS, GROUPS, GROUPS])
            w4 = work[:].rearrange("p (s a b) -> p s a b", a=GROUPS, b=GROUPS)
            v4 = work2[:].rearrange("p (s a b) -> p s a b", a=GROUPS, b=GROUPS)
            link(dve.tensor_tensor(v4, other, own, ALU.is_equal))
            tie = g.lower8[:].unsqueeze(1).to_broadcast([P, NSUBS, GROUPS * GROUPS])
            v3 = work2[:].rearrange("p (s e) -> p s e", e=EXPERTS)
            link(dve.tensor_tensor(v3, v3, tie, ALU.mult))
            link(dve.tensor_tensor(w4, other, own, ALU.is_gt))
            link(dve.tensor_tensor(work[:], work[:], work2[:], ALU.add))
            link(dve.tensor_reduce(rank[:], work[:].rearrange("p (n b) -> p n b", b=GROUPS), AX.X, ALU.add))
            link(dve.tensor_scalar(rank[:], rank[:], TOP_GROUPS - 0.5, None, ALU.is_lt))
            cg = choice[:].rearrange("p (n e) -> p n e", e=GSIZE)
            link(dve.tensor_tensor(cg, cg, rank[:].unsqueeze(2).to_broadcast([P, NG, GSIZE]), ALU.mult))
            for k in range(NSUBS):
                i = dve.max(top8[:, k, :], choice[:, k * EXPERTS:(k + 1) * EXPERTS])
            link(i)
            for k in range(NSUBS):
                e = slice(k * EXPERTS, (k + 1) * EXPERTS)
                i = dve.match_replace(work[:, e], top8[:, k, :], choice[:, e], NEG)
            link(i)
            link(dve.scalar_tensor_tensor(work[:], work[:], NEG / 2, scores[:], ALU.is_lt, ALU.mult))
            w3 = work[:].rearrange("p (s e) -> p s e", e=EXPERTS)
            link(dve.tensor_reduce(total[:], w3, AX.X, ALU.add))
            link(dve.tensor_scalar(total[:], total[:], 1e-20, None, ALU.add))
            link(dve.reciprocal(total[:], total[:]))
            link(dve.tensor_scalar(total[:], total[:], 2.5, None, ALU.mult))
            link(dve.tensor_tensor(w3, w3, total[:].unsqueeze(2).to_broadcast([P, NSUBS, EXPERTS]), ALU.mult))
            link(dve.tensor_copy(halves[:, :, 0:EXPERTS], w3))
            link(dve.tensor_tensor(v3, w3, halves[:, :, 0:EXPERTS], ALU.subtract))
            dve.tensor_scalar(halves[:, :, EXPERTS:2 * EXPERTS], v3, LOSCALE, None, ALU.mult).then_inc(halves_ready, 1)

        @block.tensor
        def _(pe):
            pe.wait_ge(halves_ready, 1)
            pe.wait_ge(scored, 4)
            for k in range(NSUBS):
                m = pe.transpose(g.bank[(k // 8) % 4].bitcast(F16)[:, (k % 8) * P:(k % 8 + 1) * P],
                                 halves[:, k, :], g.ident16[:])
                if k % 8 == 7:
                    m.then_inc(turned, 1)

        @block.sync
        def _(sp):
            for k, (src, hi, lo) in enumerate(jobs):
                if k >= 4:
                    sp.wait_ge(w_lo_ready, k - 3)
                sp.dma_start(stage[:, k % 4, 0:src.shape[1]], src).then_inc(w_loaded[k % 4], 16)

        @block.gpsimd
        def _(pool):
            for k, (src, hi, lo) in enumerate(jobs):
                pool.wait_ge(w_hi_ready, k + 1)
                pool.wait_ge(w_loaded[k % 4], 16 * (k // 4 + 1))
                pool.tensor_tensor(lo, stage[:, k % 4, 0:src.shape[1]], hi.bitcast(F32), ALU.subtract).then_inc(w_lo_ready, 1)


def experts(nc, g, tag, out_dram):
    with ExitStack() as ctx:
        def sb(n, s, d=F32): return ctx.enter_context(nc.sbuf_tensor(f"{tag}_{n}", s, d))
        def sem(n): return g.ctx.enter_context(nc.semaphore(f"{tag}_{n}"))
        xh, xl = sb("xh", [P, 2, TILE], F32R), sb("xl", [P, 2, TILE], F32R)
        act_buf = [sb(f"h{k}", [P, TILE]) for k in range(3)]
        hh = [sb(f"hh{k}", [P, TILE], F32R) for k in range(3)]
        hl = [sb(f"hl{k}", [P, TILE], F32R) for k in range(3)]
        ps_gate, ps_up, ps_w, ps_out = ([g.bank[2 * k], g.bank[2 * k + 1]] for k in range(4))
        x_loaded = [sem(f"x_loaded{u}") for u in range(2)]
        gate_up, w_ready, silu_done, t_ready, h_ready, hi_ready, lo_ready, down_done, added, stored = (
            sem(n) for n in ("gate_up", "w_ready", "silu_done", "t_ready", "h_ready", "hi_ready", "lo_ready",
                             "down_done", "added", "stored"))
        C = NCHUNKS
        block = ctx.enter_context(nc.Block())

        @block.sync
        def _(sp):
            def load(n, u):
                at = bass.ds(n * TILE, TILE)
                sp.dma_start(xh[:, u, :].bitcast(F32), g.xn_hi_dram[:, at]).then_inc(x_loaded[u], 16)
                sp.dma_start(xl[:, u, :].bitcast(F32), g.xn_lo_dram[:, at]).then_inc(x_loaded[u], 16)

            def store(n):
                if out_dram is not None:
                    sp.wait_ge(added, 1 + n + 1)
                    at = bass.ds(n * TILE, TILE)
                    sp.dma_start(out_dram[:, at], g.x_res[:, at]).then_inc(stored, 16)

            for u in range(2):
                load(u, u)
            with sp.Fori(0, NTILES // 2 - 1) as i:
                for u in range(2):
                    sp.wait_ge(gate_up, 1 + (2 * i + u + 1) * C)
                    load(2 * i + u + 2, u)
                    store(2 * i + u)
            for u in range(2):
                store(NTILES - 2 + u)
            if out_dram is not None:
                sp.wait_ge(stored, 16 * NTILES)

        @block.tensor
        def _(pe):
            pe.sem_inc(down_done, 1)
            pe.sem_inc(gate_up, 1)
            def product(out, wh, wl, rh, rl, start, stop):
                pe.matmul(out, wh, rh, start=start, stop=False)
                pe.matmul(out, wh, rl, start=False, stop=False)
                return pe.matmul(out, wl, rh, start=False, stop=stop)

            with pe.Fori(0, NTILES // 2) as i:
                base = 2 * i * C
                for step in range(2 * C + 2):
                    if step < 2 * C:
                        u, c = divmod(step, C)
                        r0, rows = chunk_rows(c)
                        if c == 0:
                            pe.wait_ge(x_loaded[u], 32 * i + 32)
                        pe.wait_ge(silu_done, 1 + base + max(step - 1, 0))
                        product(ps_gate[step % 2][0:rows, :], g.wg_hi[:, r0:r0 + rows], g.wg_lo[:, r0:r0 + rows],
                                xh[:, u, :], xl[:, u, :], True, True)
                        pe.wait_ge(h_ready, 1 + base + max(step - 1, 0))
                        product(ps_up[step % 2][0:rows, :], g.wu_hi[:, r0:r0 + rows], g.wu_lo[:, r0:r0 + rows],
                                xh[:, u, :], xl[:, u, :], True, True).then_inc(gate_up, 1)
                        if c < RCHUNKS:
                            pe.matmul(ps_w[step % 2], g.selector[:, r0:r0 + P],
                                      g.wT[:, bass.ds((2 * i + u) * TILE, TILE)],
                                      start=True, stop=True).then_inc(w_ready, 1)
                    if step >= 2:
                        j = step - 2
                        u, d = divmod(j, C)
                        rows = chunk_rows(d)[1]
                        pe.wait_ge(lo_ready, 1 + base + j + 1)
                        if d == 0:
                            pe.wait_ge(added, 1 + 2 * i)
                        product(ps_out[u], g.wd_hi[0:rows, d, :], g.wd_lo[0:rows, d, :],
                                hh[j % 3][0:rows, :], hl[j % 3][0:rows, :], d == 0, d == C - 1).then_inc(down_done, 1)

        @block.scalar
        def _(act):
            act.sem_inc(silu_done, 1)
            with act.Fori(0, NTILES // 2) as i:
                base = 2 * i * C
                for step in range(2 * C + 1):
                    if step < 2 * C:
                        rows = chunk_rows(step % C)[1]
                        act.wait_ge(gate_up, 1 + base + step + 1)
                        act.wait_ge(lo_ready, 1 + base + max(step - 2, 0))
                        act.activation(act_buf[step % 3][0:rows, :], ps_gate[step % 2][0:rows, :],
                                       ACT.Silu).then_inc(silu_done, 1)
                    if step >= 1:
                        j = step - 1
                        rows = chunk_rows(j % C)[1]
                        act.wait_ge(h_ready, 1 + base + j + 1)
                        act.wait_ge(down_done, 1 + base + max(j - 2, 0))
                        act.activation(hh[j % 3][0:rows, :], act_buf[j % 3][0:rows, :], ACT.Copy).then_inc(hi_ready, 1)

        @block.vector
        def _(dve):
            dve.sem_inc(h_ready, 1)
            dve.sem_inc(lo_ready, 1)
            dve.sem_inc(added, 1)
            with dve.Fori(0, NTILES // 2) as i:
                base = 2 * i * C
                for step in range(2 * C + 4):
                    u, c = divmod(step, C)
                    if step < 2 * C:
                        rows = chunk_rows(c)[1]
                        h = act_buf[step % 3][0:rows, :]
                        dve.wait_ge(silu_done, 1 + base + step + 1)
                        t = dve.tensor_tensor(h, ps_up[step % 2][0:rows, :], h, ALU.mult)
                        t.then_inc(t_ready if c < RCHUNKS else h_ready, 1)
                    if 1 <= step <= 2 * C:
                        j = step - 1
                        rows = chunk_rows(j % C)[1]
                        dve.wait_ge(hi_ready, base + j + 1)
                        dve.wait_ge(down_done, 1 + base + max(j - 2, 0))
                        dve.tensor_tensor(hl[j % 3][0:rows, :], act_buf[j % 3][0:rows, :],
                                          hh[j % 3][0:rows, :].bitcast(F32), ALU.subtract).then_inc(lo_ready, 1)
                    if step < 2 * C and c < RCHUNKS:
                        routed = (2 * i + u) * RCHUNKS + c + 1
                        dve.wait_ge(t_ready, routed)
                        dve.wait_ge(w_ready, routed)
                        dve.tensor_tensor(h, ps_w[step % 2], h, ALU.mult).then_inc(h_ready, 1)
                    if c == 3 and step > C:
                        dve.wait_ge(down_done, 1 + base + u * C)
                        x = g.x_res[:, bass.ds((2 * i + u - 1) * TILE, TILE)]
                        dve.tensor_tensor(x, ps_out[u - 1], x, ALU.add).then_inc(added, 1)


def flow_attention(nc, g, tag):
    with ExitStack() as ctx:
        def sb(n, s, d=F32): return ctx.enter_context(nc.sbuf_tensor(f"{tag}_{n}", s, d))
        def sem(n): return g.ctx.enter_context(nc.semaphore(f"{tag}_{n}"))
        xa = sb("xa", [P, TILE])
        qk = sb("qk", [P, 4, 2 * D])
        qke = sb("qke", [P, 4, 2 * D])
        dots = sb("dots", [P, 8 * D])
        flow = sb("flow", [P, 4, 2 * D])
        v = sb("v", [P, 4, D])
        qs = sb("qs", [P, 4, D])
        kv = sb("kv", [P, 4, HEADS * HD * HD])
        o = sb("o", [P, 4, D])
        oT = sb("oT", [P, TILE])
        inv = sb("inv", [P, 4, 2 * HEADS])
        invn = sb("invn", [P, 4, 2 * HEADS])
        cons = sb("cons", [P, 4, 2 * HEADS])
        cs = sb("cs", [P, 4, HEADS])
        alloc = sb("alloc", [P, 4, HEADS])
        comp = sb("comp", [P, 4, HEADS])
        ps_qk = g.psum[:, 0:1024]
        ps_cum = g.psum[:, 1024:2048]
        ps_kv = [g.psum[:, 2048:3072], g.psum[:, 0:1024]]
        ps_v, ps_oT = g.bank[6], g.bank[6]
        ps_cs, ps_proj = g.bank[7][:, 0:4 * HEADS], g.bank[7]
        (x_loaded, qkv_ready, qk_ready, v_copied, cum_ready, dots_ready, flow_ready, fcum_ready, cons_ready, cs_ready,
         alloc_ready, ccum_ready, vs_ready, qs_ready, kv_ready, kvcum_ready, mixed, o_ready, oT_ready, oT_copied,
         proj_ready, added, chain) = (sem(n) for n in (
             "x_loaded", "qkv_ready", "qk_ready", "v_copied", "cum_ready", "dots_ready", "flow_ready", "fcum_ready",
             "cons_ready", "cs_ready", "alloc_ready", "ccum_ready", "vs_ready", "qs_ready", "kv_ready", "kvcum_ready",
             "mixed", "o_ready", "oT_ready", "oT_copied", "proj_ready", "added", "chain"))
        NLINKS = 9
        block = ctx.enter_context(nc.Block())

        def cols(s):
            t, b = s // 2, s % 2
            return slice(b * SEQ + t * P, b * SEQ + (t + 1) * P)

        @block.sync
        def _(sp):
            with sp.Fori(0, NTILES) as i:
                sp.wait_ge(qkv_ready, 1 + i)
                sp.dma_start(xa[:], g.xn_dram[:, bass.ds(i * TILE, TILE)]).then_inc(x_loaded, 16)

        @block.tensor
        def _(pe):
            pe.sem_inc(qkv_ready, 1)
            def running(out, src):
                pe.matmul(out[0], g.tri[:], src[0], start=True, stop=True)
                pe.matmul(out[1], g.tri[:], src[1], start=True, stop=False)
                return pe.matmul(out[1], g.ones[:], src[0], start=False, stop=True)

            with pe.Fori(0, NTILES) as i:
                pe.wait_ge(x_loaded, 16 * i + 16)
                for s in range(4):
                    x = xa[:, cols(s)]
                    for out, w0, w1 in ((ps_qk[:, s * 256:(s + 1) * 256], 0, 256), (ps_v[:, s * P:(s + 1) * P], 256, 384)):
                        pe.matmul(out, x, g.wqkv_a[:, w0:w1], start=True, stop=False)
                        m = pe.matmul(out, g.ones[0:1, :], g.bqkv_a[:, w0:w1], start=False, stop=True)
                m.then_inc(qkv_ready, 1)
                pe.wait_ge(qk_ready, i + 1)
                halves = [qk[:, 2 * t:2 * t + 2, :] for t in range(2)]
                running([ps_cum[:, 0:512], ps_cum[:, 512:1024]], halves).then_inc(cum_ready, 1)
                pe.wait_ge(flow_ready, i + 1)
                halves = [flow[:, 2 * t:2 * t + 2, :] for t in range(2)]
                running([ps_cum[:, 0:512], ps_cum[:, 512:1024]], halves).then_inc(fcum_ready, 1)
                pe.wait_ge(cs_ready, i + 1)
                pe.wait_ge(added, 1 + i)
                running([ps_cs[:, 0:32], ps_cs[:, 32:64]], [cs[:, 2 * t:2 * t + 2, :] for t in range(2)]).then_inc(ccum_ready, 1)
                for s in range(4):
                    t, b = s // 2, s % 2
                    pe.wait_ge(kv_ready, 4 * i + s + 1)
                    if s >= 2:
                        pe.wait_ge(mixed, 4 * i + s - 1)
                    for c in range(2):
                        at = slice(c * 512, (c + 1) * 512)
                        out = ps_kv[s % 2][:, at]
                        m = pe.matmul(out, g.tri[:], kv[:, s, at], start=True, stop=(t == 0))
                        if t == 1:
                            m = pe.matmul(out, g.ones[:], kv[:, b, at], start=False, stop=True)
                    m.then_inc(kvcum_ready, 1)
                pe.wait_ge(o_ready, 4 * i + 4)
                pe.wait_ge(v_copied, i + 1)
                for s in range(4):
                    m = pe.transpose(ps_oT[:, cols(s)], o[:, s, :], g.ident[:])
                m.then_inc(oT_ready, 1)
                pe.wait_ge(oT_copied, i + 1)
                pe.matmul(ps_proj, g.wo_a[:], oT[:], start=True, stop=True).then_inc(proj_ready, 1)

        @block.scalar
        def _(act):
            with act.Fori(0, NTILES) as i:
                act.wait_ge(qkv_ready, 1 + i + 1)
                act.activation(qk[:].rearrange("p s d -> p (s d)"), ps_qk, ACT.Sigmoid).then_inc(qk_ready, 1)
                act.activation(v[:].rearrange("p s d -> p (s d)"), ps_v, ACT.Copy).then_inc(v_copied, 1)
                act.wait_ge(cons_ready, i + 1)
                act.activation(alloc[:], cons[:, :, HEADS:2 * HEADS], ACT.Sigmoid).then_inc(alloc_ready, 1)
                act.activation(cs[:], cons[:, :, 0:HEADS], ACT.Exp).then_inc(cs_ready, 1)
                act.wait_ge(oT_ready, i + 1)
                act.activation(oT[:], ps_oT, ACT.Copy).then_inc(oT_copied, 1)

        @block.vector
        def _(dve):
            dve.sem_inc(added, 1)
            with dve.Fori(0, NTILES) as i:
                steps = [0]

                def link(ins):
                    steps[0] += 1
                    ins.then_inc(chain, 1)
                    dve.wait_ge(chain, i * NLINKS + steps[0])

                def by_head(ap):
                    return ap.rearrange("p (n d) -> p n d", d=HD)

                def over_head(small):
                    return small.unsqueeze(3).to_broadcast([P, 4, HEADS, HD])

                def heads(ap):
                    return ap.rearrange("p s (h d) -> p s h d", d=HD)

                dve.wait_ge(qk_ready, i + 1)
                dve.tensor_scalar(qke[:, :, 0:D], qk[:, :, D:2 * D], FLOW_EPS, None, ALU.add)
                link(dve.tensor_scalar(qke[:, :, D:2 * D], qk[:, :, 0:D], FLOW_EPS, None, ALU.add))
                dve.wait_ge(cum_ready, i + 1)
                dve.scalar_tensor_tensor(dots[:], ps_cum, FLOW_EPS, qke[:].rearrange("p s d -> p (s d)"),
                                         ALU.add, ALU.mult).then_inc(dots_ready, 1)
                dve.wait_ge(dots_ready, 2 * i + 1)
                flat = inv[:].rearrange("p s h -> p (s h)")
                link(dve.tensor_reduce(flat, by_head(dots[:]), AX.X, ALU.add))
                link(dve.reciprocal(flat, flat))
                link(dve.tensor_tensor(invn[:], inv[:], g.normal[:], ALU.mult))
                dve.tensor_tensor(heads(flow[:, :, 0:D]), heads(qk[:, :, 0:D]), over_head(invn[:, :, HEADS:2 * HEADS]), ALU.mult)
                dve.tensor_tensor(heads(flow[:, :, D:2 * D]), heads(qk[:, :, D:2 * D]), over_head(invn[:, :, 0:HEADS]),
                                  ALU.mult).then_inc(flow_ready, 1)
                dve.wait_ge(fcum_ready, i + 1)
                dve.scalar_tensor_tensor(dots[:], ps_cum, FLOW_EPS, qke[:].rearrange("p s d -> p (s d)"),
                                         ALU.add, ALU.mult).then_inc(dots_ready, 1)
                dve.wait_ge(dots_ready, 2 * i + 2)
                link(dve.tensor_reduce(cons[:].rearrange("p s h -> p (s h)"), by_head(dots[:]), AX.X, ALU.add))
                dve.tensor_tensor(cons[:], cons[:], g.inv_normal[:], ALU.mult).then_inc(cons_ready, 1)
                dve.wait_ge(alloc_ready, i + 1)
                link(dve.tensor_tensor(alloc[:], alloc[:], inv[:, :, HEADS:2 * HEADS], ALU.mult))
                dve.tensor_tensor(heads(qs[:]), heads(qk[:, :, 0:D]), over_head(alloc[:]), ALU.mult).then_inc(qs_ready, 1)
                dve.wait_ge(ccum_ready, i + 1)
                dve.wait_ge(cs_ready, i + 1)
                flat_comp = comp[:].rearrange("p s h -> p (s h)")
                link(dve.reciprocal(flat_comp, ps_cs))
                link(dve.tensor_tensor(flat_comp, flat_comp, cs[:].rearrange("p s h -> p (s h)"), ALU.mult))
                link(dve.tensor_tensor(comp[:], comp[:], g.normal[:, :, 0:HEADS], ALU.mult))
                dve.wait_ge(v_copied, i + 1)
                dve.tensor_tensor(heads(v[:]), heads(v[:]), over_head(comp[:]), ALU.mult).then_inc(vs_ready, 1)
                dve.wait_ge(qs_ready, i + 1)
                for s in range(4):
                    dve.wait_ge(kvcum_ready, 4 * i + s + 1)
                    q4 = qs[:, s, :].rearrange("p (h d) -> p h d", d=HD).unsqueeze(2).to_broadcast([P, HEADS, HD, HD])
                    dve.tensor_tensor(dots[:].rearrange("p (h m d) -> p h m d", m=HD, d=HD),
                                      ps_kv[s % 2].rearrange("p (h m d) -> p h m d", m=HD, d=HD), q4, ALU.mult).then_inc(mixed, 1)
                    dve.wait_ge(mixed, 4 * i + s + 1)
                    dve.tensor_reduce(o[:, s, :], by_head(dots[:]), AX.X, ALU.add).then_inc(o_ready, 1)
                    dve.wait_ge(o_ready, 4 * i + s + 1)
                dve.wait_ge(proj_ready, i + 1)
                x = g.x_res[:, bass.ds(i * TILE, TILE)]
                dve.scalar_tensor_tensor(x, ps_proj, g.bo_a[:, 0:1], x, ALU.add, ALU.add).then_inc(added, 1)
                assert steps[0] == NLINKS, steps

        @block.gpsimd
        def _(pool):
            with pool.Fori(0, NTILES) as i:
                for s in range(4):
                    if s == 0:
                        pool.wait_ge(vs_ready, i + 1)
                    v4 = v[:, s, :].rearrange("p (h m) -> p h m", m=HD).unsqueeze(3).to_broadcast([P, HEADS, HD, HD])
                    k4 = qk[:, s, D:2 * D].rearrange("p (h d) -> p h d", d=HD).unsqueeze(2).to_broadcast([P, HEADS, HD, HD])
                    pool.tensor_tensor(kv[:, s, :].rearrange("p (h m d) -> p h m d", m=HD, d=HD), v4, k4, ALU.mult).then_inc(kv_ready, 1)


def softmax_attention(nc, g, tag):
    with ExitStack() as ctx:
        def sb(n, s, d=F32): return ctx.enter_context(nc.sbuf_tensor(f"{tag}_{n}", s, d))
        def sem(n): return g.ctx.enter_context(nc.semaphore(f"{tag}_{n}"))
        xa = sb("xa", [P, TILE])
        q_st = sb("q_st", [P, QUADS, TILE], F32R)
        k_st = sb("k_st", [P, QUADS, TILE], F32R)
        plain = sb("plain", [P, 2, TILE])
        signed = sb("signed", [P, 2, TILE], F32R)
        vv = sb("vv", [P, 4, HEADS, 32])
        avT = sb("avT", [P, 4, SEQ])
        negmax = sb("negmax", [P, 2, 2, HEADS])
        maxrows = sb("maxrows", [P, 2, 2, HEADS, 32])
        prob = sb("prob", [P, 2, 1536])
        o = sb("o", [P, 4, D])
        inv = sb("inv", [P, 2 * HEADS])
        oT = sb("oT", [P, TILE])
        ring = [g.psum[:, 0:1536], g.psum[:, 1536:3072]]
        (x_loaded, st_raw, st_plain, st_signed, st_ready, v_raw, v_ready, s_ready, m_ready, mrow_ready, mT_ready,
         q_ready, sT_ready, p_ready, av_ready, o_ready, oT_ready, oT_copied, proj_ready, added, chain) = (
             sem(n) for n in ("x_loaded", "st_raw", "st_plain", "st_signed", "st_ready", "v_raw", "v_ready", "s_ready",
                              "m_ready", "mrow_ready", "mT_ready", "q_ready", "sT_ready", "p_ready", "av_ready",
                              "o_ready", "oT_ready", "oT_copied", "proj_ready", "added", "chain"))
        cleared, av_copied, avT_turned = sem("cleared"), sem("av_copied"), sem("avT_turned")
        NST = 2 * QUADS
        NLINKS = 4
        block = ctx.enter_context(nc.Block())

        def sub(b, t):
            return slice(b * SEQ + t * P, b * SEQ + (t + 1) * P)

        @block.sync
        def _(sp):
            with sp.Fori(0, NTILES) as i:
                sp.wait_ge(v_raw, 1 + i)
                sp.dma_start(xa[:], g.xn_dram[:, bass.ds(i * TILE, TILE)]).then_inc(x_loaded, 16)

        @block.gpsimd
        def _(pool):
            pool.memset(maxrows[:], 0.0).then_inc(cleared, 1)
            pool.memset(vv[:, :, :, HD:], 0.0).then_inc(cleared, 1)
            pool.wait_ge(cleared, 2)
            pool.memset(vv[:, :, :, HD], 1.0).then_inc(cleared, 1)

        def turn(pe, i, b):
            pe.wait_ge(av_copied, (2 * i + b + 1) * QUADS)
            for t in range(2):
                for q in range(4):
                    m = pe.transpose(g.bank[6 + t][:, q * P:(q + 1) * P], avT[:, q, t * P:(t + 1) * P], g.ident[:])
            m.then_inc(avT_turned, 1)

        @block.tensor
        def _(pe):
            pe.sem_inc(v_raw, 1)
            with pe.Fori(0, NTILES) as i:
                pe.wait_ge(x_loaded, 16 * i + 16)
                for n in range(NST):
                    if n >= 2:
                        pe.wait_ge(st_plain, i * NST + n - 1)
                    w = g.wq_b if n < QUADS else g.wk_b
                    pe.matmul(ring[n % 2][:, 0:512], w[:, n % QUADS, :], xa[:], start=True, stop=True).then_inc(st_raw, 1)
                pe.wait_ge(added, 1 + i)
                for s in range(4):
                    at = g.bank[7][:, s * P:(s + 1) * P]
                    pe.matmul(at, xa[:, s * P:(s + 1) * P], g.wv_b[:], start=True, stop=False)
                    m = pe.matmul(at, g.ones[0:1, :], g.bv_b[:], start=False, stop=True)
                m.then_inc(v_raw, 1)
                for b in range(2):
                    pe.wait_ge(st_ready, NST * i + NST)
                    for q in range(QUADS):
                        unit = (2 * i + b) * QUADS + q
                        r = ring[q % 2]
                        if b == 0 and q < 2:
                            pe.wait_ge(st_plain, NST * i + NST)
                        else:
                            pe.wait_ge(m_ready, unit - 1)
                        pe.matmul(r[:, 0:512], g.ident_b[:], g.mask_key[:, 0:512], start=True, stop=False)
                        pe.matmul(r[:, 512:1024], g.ident_b[:], g.mask_key[:, 512:1024], start=True, stop=False)
                        pe.matmul(r[:, 1024:1536], g.ident_b[:], g.mask_key[:, 512:1024], start=True, stop=False)
                        rows = slice(32 * q, 32 * q + 32)
                        for h in range(QUADS):
                            qa = q_st[rows, h, :]
                            ka = k_st[rows, h, :]
                            pe.matmul(r[:, h * P:(h + 1) * P], qa[:, sub(b, 0)], ka[:, sub(b, 0)], start=False, stop=(h == 3))
                            m = pe.matmul(r[:, 512 + h * 256:768 + h * 256], qa[:, sub(b, 1)], ka[:, b * SEQ:(b + 1) * SEQ],
                                          start=False, stop=(h % 2 == 1))
                        m.then_inc(s_ready, 1)
                pe.wait_ge(v_ready, i + 1)
                for b in range(2):
                    pe.wait_ge(mrow_ready, 2 * i + b + 1)
                    dst = (g.psum[:, 3072:4096], ring[0][:, 0:1024])[b]
                    for t in range(2):
                        for q in range(QUADS):
                            m = pe.transpose(dst[:, (4 * t + q) * P:(4 * t + q + 1) * P],
                                             maxrows[:, b, t, 4 * q:4 * q + 4, :].rearrange("p h r -> p (h r)"), g.ident[:])
                    m.then_inc(mT_ready, 1)
                for u in range(2 * QUADS + 1):
                    if u < 2 * QUADS:
                        b, q = u // QUADS, u % QUADS
                        r = ring[u % 2]
                        if u < 2:
                            pe.wait_ge(q_ready, 2 * i + 2)
                        else:
                            pe.wait_ge(p_ready, 2 * (2 * i * QUADS + u) - 2)
                        pe.matmul(r[:, 0:512], g.ident_b[:], g.mask_query[:, 0:512], start=True, stop=False)
                        pe.matmul(r[:, 512:1024], g.ident_b[:], g.mask_query[:, 0:512], start=True, stop=False)
                        pe.matmul(r[:, 1024:1536], g.ident_b[:], g.mask_query[:, 512:1024], start=True, stop=False)
                        rows = slice(32 * q, 32 * q + 32)
                        for h in range(QUADS):
                            qa = q_st[rows, h, :]
                            ka = k_st[rows, h, :]
                            pe.matmul(r[:, h * 256:(h + 1) * 256], ka[:, sub(b, 0)], qa[:, b * SEQ:(b + 1) * SEQ],
                                      start=False, stop=(h % 2 == 1))
                            m = pe.matmul(r[:, 1024 + h * P:1024 + (h + 1) * P], ka[:, sub(b, 1)], qa[:, sub(b, 1)],
                                          start=False, stop=(h == 3))
                        m.then_inc(sT_ready, 1)
                    if u == QUADS + 1:
                        turn(pe, i, 0)
                    if u >= 1:
                        b, q = (u - 1) // QUADS, (u - 1) % QUADS
                        unit = 2 * i * QUADS + u - 1
                        pe.wait_ge(p_ready, 2 * unit + 2)
                        if u - 1 == QUADS:
                            pe.wait_ge(o_ready, 2 * i + 1)
                        elif u - 1 >= 2:
                            pe.wait_ge(av_copied, unit - 1)
                        pr = prob[:, (u - 1) % 2, :]
                        for h in range(4):
                            head = 4 * h + q
                            out = g.bank[6 + q % 2][32 * h:32 * h + 32, 0:SEQ]
                            pe.matmul(out, vv[:, 2 * b, head, :], pr[:, h * 256:(h + 1) * 256], start=True, stop=False)
                            m = pe.matmul(out[:, P:SEQ], vv[:, 2 * b + 1, head, :], pr[:, 1024 + h * P:1024 + (h + 1) * P],
                                          start=False, stop=True)
                        m.then_inc(av_ready, 1)
                turn(pe, i, 1)
                pe.wait_ge(o_ready, 2 * i + 2)
                for s in range(4):
                    m = pe.transpose(g.bank[6][:, s * P:(s + 1) * P], o[:, s, :], g.ident[:])
                m.then_inc(oT_ready, 1)
                pe.wait_ge(oT_copied, i + 1)
                pe.matmul(g.bank[7], g.wo_b[:], oT[:], start=True, stop=True).then_inc(proj_ready, 1)

        @block.scalar
        def _(act):
            with act.Fori(0, NTILES) as i:
                for n in range(NST):
                    act.wait_ge(st_raw, i * NST + n + 1)
                    if n >= 2:
                        act.wait_ge(st_ready, i * NST + n - 1)
                    bias = (g.bq_b if n < QUADS else g.bk_b)[:, n % QUADS:n % QUADS + 1]
                    act.activation(plain[:, n % 2, :], ring[n % 2][:, 0:512], ACT.Identity, bias=bias).then_inc(st_plain, 1)
                    act.wait_ge(st_plain, i * NST + n + 1)
                    sign = g.split[:, 0:1] if n < QUADS else g.split[:, 2:3]
                    act.activation(signed[:, n % 2, :], plain[:, n % 2, :], ACT.Copy, scale=sign).then_inc(st_signed, 1)
                act.wait_ge(v_raw, 1 + i + 1)
                act.wait_ge(cleared, 3)
                act.activation(vv[:, :, :, 0:HD], g.bank[7].rearrange("p (s h d) -> p s h d", s=4, d=HD), ACT.Copy).then_inc(v_ready, 1)
                for b in range(2):
                    for q in range(QUADS):
                        unit = (2 * i + b) * QUADS + q
                        act.wait_ge(sT_ready, unit + 1)
                        if b + q >= 2 or b == 1:
                            act.wait_ge(av_ready, unit - 1)
                        act.activation(prob[:, q % 2, 0:1024], ring[q % 2][:, 0:1024], ACT.Exp, scale=SCALE).then_inc(p_ready, 1)
                        act.activation(prob[:, q % 2, 1024:1536], ring[q % 2][:, 1024:1536], ACT.Exp, scale=SCALE).then_inc(p_ready, 1)
                act.wait_ge(oT_ready, i + 1)
                act.activation(oT[:], g.bank[6], ACT.Copy).then_inc(oT_copied, 1)

        @block.vector
        def _(dve):
            dve.sem_inc(added, 1)
            with dve.Fori(0, NTILES) as i:
                steps = [0]

                def link(ins):
                    steps[0] += 1
                    ins.then_inc(chain, 1)
                    dve.wait_ge(chain, i * NLINKS + steps[0])

                for n in range(NST):
                    dve.wait_ge(st_signed, i * NST + n + 1)
                    low = g.split[:, 1:2] if n < QUADS else g.split[:, 3:4]
                    dst = (q_st if n < QUADS else k_st)[:, n % QUADS, :]
                    dve.scalar_tensor_tensor(dst, plain[:, n % 2, :], low, signed[:, n % 2, :].bitcast(F32),
                                             ALU.mult, ALU.add).then_inc(st_ready, 1)
                for b in range(2):
                    for q in range(QUADS):
                        r = ring[q % 2]
                        dve.wait_ge(s_ready, (2 * i + b) * QUADS + q + 1)
                        dve.tensor_reduce(negmax[:, b, 0, q:HEADS:4], r[:, 0:512].rearrange("p (h k) -> p h k", k=P),
                                          AX.X, ALU.max, negate=True)
                        dve.tensor_reduce(negmax[:, b, 1, q:HEADS:4], r[:, 512:1536].rearrange("p (h k) -> p h k", k=SEQ),
                                          AX.X, ALU.max, negate=True).then_inc(m_ready, 1)
                    dve.wait_ge(m_ready, (2 * i + b + 1) * QUADS)
                    dve.wait_ge(cleared, 3)
                    link(dve.tensor_copy(maxrows[:, b, :, :, 24].bitcast(F32R), negmax[:, b, :, :]))
                    dve.tensor_tensor(maxrows[:, b, :, :, 25], negmax[:, b, :, :], maxrows[:, b, :, :, 24],
                                      ALU.subtract).then_inc(mrow_ready, 1)
                for b in range(2):
                    dve.wait_ge(mT_ready, 2 * i + b + 1)
                    src = (g.psum[:, 3072:4096], ring[0][:, 0:1024])[b]
                    for t in range(2):
                        qa = q_st[:, :, sub(b, t)]
                        m = dve.tensor_tensor(qa, src[:, t * 512:(t + 1) * 512].rearrange("p (q k) -> p q k", k=P),
                                              qa.bitcast(F32), ALU.add)
                    m.then_inc(q_ready, 1)
                for b in range(2):
                    for q in range(4):
                        dve.wait_ge(av_ready, (2 * i + b) * QUADS + q + 1)
                        dve.tensor_copy(avT[:, q, :], g.bank[6 + q % 2][:, 0:SEQ]).then_inc(av_copied, 1)
                    dve.wait_ge(avT_turned, 2 * i + b + 1)
                    av = g.psum[:, 3072:4096].rearrange("p (n e) -> p n e", e=32)
                    link(dve.reciprocal(inv[:], av[:, :, HD]))
                    for t in range(2):
                        m = dve.tensor_tensor(
                            o[:, 2 * b + t, :].rearrange("p (h q d) -> p q h d", q=4, d=HD),
                            av[:, t * HEADS:(t + 1) * HEADS, 0:HD].rearrange("p (q h) d -> p q h d", q=4),
                            inv[:, t * HEADS:(t + 1) * HEADS].rearrange("p (q h) -> p q h", q=4).unsqueeze(3).to_broadcast([P, 4, 4, HD]),
                            ALU.mult)
                    m.then_inc(o_ready, 1)
                dve.wait_ge(proj_ready, i + 1)
                x = g.x_res[:, bass.ds(i * TILE, TILE)]
                dve.scalar_tensor_tensor(x, g.bank[7], g.bo_b[:, 0:1], x, ALU.add, ALU.add).then_inc(added, 1)
                assert steps[0] == NLINKS, steps


def setup(nc, g, ins, tag, first):
    with ExitStack() as ctx:
        def sem(n): return g.ctx.enter_context(nc.semaphore(f"{tag}_{n}"))
        loaded, made, inverted = sem("loaded"), sem("made"), sem("inverted")
        iota = ctx.enter_context(nc.sbuf_tensor(f"{tag}_iota", [P, 4 * 2 * HEADS], I32))
        normal_step = []
        block = ctx.enter_context(nc.Block())

        @block.sync
        def _(sp):
            pairs = [(g.x_res[:], ins["xT"]), (g.gate_wT[:], ins["gate_wT"]),
                     (g.gate_bias[:], ins["gate_bias"].partition_broadcast(P)),
                     (g.lower8[:], ins["lower8"].partition_broadcast(P))] if first else []
            pairs += [
                     (g.wqkv_a[:], ins["wqkv_a"]), (g.bqkv_a[:], ins["bqkv_a"]), (g.wo_a[:], ins["wo_a"]),
                     (g.bo_a[:], ins["bo_a"]), (g.wq_b[:], ins["wq_b"]), (g.wk_b[:], ins["wk_b"]),
                     (g.wv_b[:], ins["wv_b"]), (g.bv_b[:], ins["bv_b"]), (g.wo_b[:], ins["wo_b"]),
                     (g.bo_b[:], ins["bo_b"]), (g.bq_b[:], ins["bq_b"]), (g.bk_b[:], ins["bk_b"]),
                     (g.split[:], ins["split"])]
            for dst, src in pairs:
                sp.dma_start(dst, src).then_inc(loaded, 16)
            sp.wait_ge(loaded, 16 * len(pairs))

        @block.gpsimd
        def _(pool):
            k = [0]

            def then(ins):
                k[0] += 1
                ins.then_inc(made, 1)
                pool.wait_ge(made, k[0])

            then(pool.memset(g.ones[:], 1.0))
            then(pool.memset(g.ones_d[:], 1.0 / D))
            then(pool.memset(g.ln_eps[:], LN_EPS))
            then(pool.memset(g.ident_f[:], 1.0))
            then(pool.affine_select(out=g.ident[:], in_=g.ident_f[:], compare_op=ALU.is_equal, fill=0.0, base=0,
                                    pattern=[[-1, P]], channel_multiplier=1))
            then(pool.affine_select(out=g.tri[:], in_=g.ident_f[:], compare_op=ALU.is_ge, fill=0.0, base=0,
                                    pattern=[[1, P]], channel_multiplier=-1))
            then(pool.tensor_copy(g.ident16[:], g.ident[:]))
            then(pool.tensor_copy(g.ident_b[:], g.ident[:]))
            then(pool.memset(g.mask_key[:], 0.0))
            then(pool.memset(g.mask_query[:], 0.0))
            first = g.mask_key[:, 0:512].rearrange("p (h k) -> p h k", k=P)
            then(pool.affine_select(out=first, in_=first, compare_op=ALU.is_ge, fill=NEG, base=0,
                                    pattern=[[0, 4], [-1, P]], channel_multiplier=1))
            second = g.mask_key[:, 512:1024].rearrange("p (h t k) -> p h t k", t=2, k=P)[:, :, 1, :]
            then(pool.affine_select(out=second, in_=second, compare_op=ALU.is_ge, fill=NEG, base=0,
                                    pattern=[[0, 2], [-1, P]], channel_multiplier=1))
            first = g.mask_query[:, 0:512].rearrange("p (h t k) -> p h t k", t=2, k=P)[:, :, 0, :]
            then(pool.affine_select(out=first, in_=first, compare_op=ALU.is_ge, fill=NEG, base=0,
                                    pattern=[[0, 2], [1, P]], channel_multiplier=-1))
            second = g.mask_query[:, 512:1024].rearrange("p (h k) -> p h k", k=P)
            then(pool.affine_select(out=second, in_=second, compare_op=ALU.is_ge, fill=NEG, base=0,
                                    pattern=[[0, 4], [1, P]], channel_multiplier=-1))
            then(pool.iota(iota[:], pattern=[[P, 2], [0, 4 * HEADS]], base=1, channel_multiplier=1))
            then(pool.tensor_copy(g.normal[:].rearrange("p s h -> p (s h)"), iota[:]))
            normal_step.append(k[0])


        @block.vector
        def _(dve):
            dve.wait_ge(made, normal_step[0])
            dve.reciprocal(g.inv_normal[:], g.normal[:]).then_inc(inverted, 1)


def split_down_weights(nc, g, ins, tag):
    with ExitStack() as ctx:
        stage = ctx.enter_context(nc.sbuf_tensor(f"{tag}_stage", [P, 4, SPLIT_COLS], F32))
        jobs = []
        per = SPLIT_COLS // D
        for a in range(0, RCHUNKS, per):
            n = min(per, RCHUNKS - a)
            src = ins["wd"][a * P:(a + n) * P, :].rearrange("(c p) d -> p c d", p=P)
            jobs.append((P, n * D, src, g.wd_hi[:, a:a + n, :], g.wd_lo[:, a:a + n, :]))
        src = ins["wd"][ROUTED:, :].rearrange("(c p) d -> p c d", p=INNER)
        jobs.append((INNER, 2 * D, src, g.wd_hi[0:INNER, RCHUNKS:, :], g.wd_lo[0:INNER, RCHUNKS:, :]))
        loaded, hi_ready, lo_ready, first = g.w_loaded, g.w_hi_ready, g.w_lo_ready, g.jobs_done
        assert first % 4 == 0
        block = ctx.enter_context(nc.Block())

        def shaped(k, rows, n, like):
            s = stage[0:rows, k % 4, 0:n]
            return s if len(like.shape) == 2 else s.rearrange("p (c d) -> p c d", d=D)

        @block.sync
        def _(sp):
            for k, (rows, n, src, hi, lo) in enumerate(jobs, first):
                if k >= first + 4:
                    sp.wait_ge(lo_ready, k - 3)
                sp.dma_start(shaped(k, rows, n, hi), src).then_inc(loaded[k % 4], 16)

        @block.scalar
        def _(act):
            for k, (rows, n, src, hi, lo) in enumerate(jobs, first):
                act.wait_ge(loaded[k % 4], 16 * (k // 4 + 1))
                act.activation(hi, shaped(k, rows, n, hi), ACT.Copy).then_inc(hi_ready, 1)

        @block.vector
        def _(dve):
            for k, (rows, n, src, hi, lo) in enumerate(jobs, first):
                dve.wait_ge(hi_ready, k + 1)
                dve.wait_ge(loaded[k % 4], 16 * (k // 4 + 1))
                dve.tensor_tensor(lo, shaped(k, rows, n, hi), hi.bitcast(F32), ALU.subtract).then_inc(lo_ready, 1)


def build(nc, ins, outT):
    with ExitStack() as ctx:
        g = Shared()
        g.ctx = ctx
        def sb(n, s, d=F32): return ctx.enter_context(nc.sbuf_tensor(n, s, d))
        g.psum = ctx.enter_context(nc.psum_tensor("psum", [P, 8 * 512], F32))
        g.bank = [g.psum[:, k * 512:(k + 1) * 512] for k in range(8)]
        g.x_res = sb("x_res", [P, TOKENS])
        R = ROUTED + SHARED
        g.gate_wT, g.gate_bias, g.lower8 = sb("gate_wT", [P, EXPERTS]), sb("gate_bias", [P, EXPERTS]), sb("lower8", [P, 64])
        g.wo_b, g.bo_b = sb("wo_b", [P, D]), sb("bo_b", [P, 1])
        g.ones, g.ones_d, g.ident, g.ident16, g.ln_eps = sb("ones", [P, P]), sb("ones_d", [P, P]), sb("ident", [P, P]), sb("ident16", [P, P], F16), sb("ln_eps", [P, 1])
        g.xn_dram = nc.dram_tensor("xn_scratch", [P, TOKENS], F32, kind="Internal").ap()
        g.xn_hi_dram = nc.dram_tensor("xn_hi_scratch", [P, TOKENS], F32, kind="Internal").ap()
        g.xn_lo_dram = nc.dram_tensor("xn_lo_scratch", [P, TOKENS], F32, kind="Internal").ap()

        def constants(c2, tag):
            def sc(n, s, d=F32): return c2.enter_context(nc.sbuf_tensor(f"{tag}_{n}", s, d))
            g.wqkv_a, g.bqkv_a, g.wo_a, g.bo_a = sc("wqkv_a", [P, 3 * D]), sc("bqkv_a", [1, 3 * D]), sc("wo_a", [P, D]), sc("bo_a", [P, 1])
            g.wq_b, g.wk_b = sc("wq_b", [P, QUADS, P]), sc("wk_b", [P, QUADS, P])
            g.bq_b, g.bk_b, g.split = sc("bq_b", [P, QUADS]), sc("bk_b", [P, QUADS]), sc("split", [P, 4])
            g.wv_b, g.bv_b = sc("wv_b", [P, D]), sc("bv_b", [1, D])
            g.tri, g.ident_f, g.ident_b = sc("tri", [P, P]), sc("ident_f", [P, P]), sc("ident_b", [P, P], BF16)
            g.mask_key, g.mask_query = sc("mask_key", [P, 1024], BF16), sc("mask_query", [P, 1024], BF16)
            g.normal, g.inv_normal = sc("normal", [P, 4, 2 * HEADS]), sc("inv_normal", [P, 4, 2 * HEADS])

        def gate_up_weights(c2, tag):
            def sc(n, s, d=F32): return c2.enter_context(nc.sbuf_tensor(f"{tag}_{n}", s, d))
            g.wg_hi, g.wg_lo, g.wu_hi, g.wu_lo = (sc(n, [P, R], F32R) for n in ("wg_hi", "wg_lo", "wu_hi", "wu_lo"))

        def down_weights(c2, tag):
            def sc(n, s, d=F32): return c2.enter_context(nc.sbuf_tensor(f"{tag}_{n}", s, d))
            g.wd_hi, g.wd_lo = (sc(n, [P, NCHUNKS, D], F32R) for n in ("wd_hi", "wd_lo"))

        def moe(tag, out_dram):
            with ExitStack() as c3:
                g.wT = c3.enter_context(nc.sbuf_tensor(f"{tag}_wT", [P, TOKENS], F16))
                g.selector = c3.enter_context(nc.sbuf_tensor(f"{tag}_selector", [P, ROUTED], F16))
                layernorm(nc, g, f"{tag}_ln", True)
                gate_up_weights(c3, tag)
                routing(nc, g, ins, f"{tag}_route")
                down_weights(c3, tag)
                split_down_weights(nc, g, ins, f"{tag}_split")
                experts(nc, g, f"{tag}_exp", out_dram)

        with ExitStack() as keep:
            constants(keep, "flow")
            setup(nc, g, ins, "flow_setup", True)
            layernorm(nc, g, "flow_ln", False)
            flow_attention(nc, g, "flow")
        moe("moe1", None)
        with ExitStack() as keep:
            constants(keep, "attn")
            setup(nc, g, ins, "attn_setup", False)
            layernorm(nc, g, "attn_ln", False)
            softmax_attention(nc, g, "attn")
        moe("moe2", outT)


def lay_out(a):
    f = np.float32
    def cat(*x): return np.ascontiguousarray(np.concatenate(x, axis=0))
    cw, cb = np.asarray(a["L0_attn_b_c_attn_w"]), np.asarray(a["L0_attn_b_c_attn_b"])

    def stack(w, b, ones):
        ws, bs = np.zeros((D, QUADS, 4, 4, HD), f), np.zeros((QUADS, 4, 4, HD), f)
        for r in range(3):
            ws[:, :, :, r, :] = w.reshape(D, QUADS, 4, HD)
            bs[:, :, r, :] = b.reshape(QUADS, 4, HD)
        if ones:
            bs[:, :, 3, 0:2] = 1.0
        return ws.reshape(D, QUADS, P), np.ascontiguousarray(bs.reshape(QUADS, P).T)

    wq, bq = stack(cw[:, 0:D], cb[0:D], False)
    wk, bk = stack(cw[:, D:2 * D], cb[D:2 * D], True)
    split = np.zeros((4, 4, HD, 4), f)
    split[..., 0], split[..., 2] = 1.0, 1.0
    split[:, 2, :, 0], split[:, 2, :, 1] = -1.0, 1.0
    split[:, 1, :, 2], split[:, 1, :, 3] = -1.0, 1.0
    x = np.asarray(a["L0_attn_a_x"]).reshape(TOKENS, D)
    return {
        "xT": np.ascontiguousarray(x.T),
        "wqkv_a": np.ascontiguousarray(np.concatenate([a["L0_attn_a_Wq"], a["L0_attn_a_Wk"], a["L0_attn_a_Wv"]], axis=1)),
        "bqkv_a": np.concatenate([a["L0_attn_a_bq"], a["L0_attn_a_bk"], a["L0_attn_a_bv"]]).reshape(1, 3 * D),
        "wo_a": np.asarray(a["L0_attn_a_Wo"]), "bo_a": np.asarray(a["L0_attn_a_bo"]).reshape(D, 1),
        "wq_b": wq, "wk_b": wk, "bq_b": bq, "bk_b": bk, "split": split.reshape(P, 4),
        "wv_b": np.ascontiguousarray(cw[:, 2 * D:]), "bv_b": cb[2 * D:].reshape(1, D),
        "wo_b": np.asarray(a["L0_attn_b_c_proj_w"]), "bo_b": np.asarray(a["L0_attn_b_c_proj_b"]).reshape(D, 1),
        "gate_wT": np.ascontiguousarray(np.asarray(a["L0_ffn_gate_w"]).T),
        "gate_bias": np.asarray(a["L0_ffn_gate_bias"]),
        "lower8": np.tril(np.ones((8, 8), f), -1).reshape(64),
        "wg": np.ascontiguousarray(cat(np.asarray(a["L0_ffn_Wg"]).reshape(ROUTED, D), a["L0_ffn_Sg"]).T),
        "wu": np.ascontiguousarray(cat(np.asarray(a["L0_ffn_Wu"]).reshape(ROUTED, D), a["L0_ffn_Su"]).T),
        "wd": cat(np.asarray(a["L0_ffn_Wd"]).transpose(0, 2, 1).reshape(ROUTED, D), np.asarray(a["L0_ffn_Sd"]).T),
    }


def kernel(**inputs):
    import concourse.bacc as _bacc
    from concourse.bass_utils import run_bass_kernel_spmd as _run

    nc = _bacc.Bacc("TRN2", target_bir_lowering=False, num_devices=1)
    arrays, ins = {}, {}
    for name, a in lay_out(inputs).items():
        arrays[f"in_{name}_dram"] = a
        ins[name] = nc.dram_tensor(f"in_{name}_dram", a.shape, mybir.dt.from_np(a.dtype), kind="ExternalInput").ap()
    outT = nc.dram_tensor("outT_dram", (D, TOKENS), F32, kind="ExternalOutput").ap()
    build(nc, ins, outT)
    r = _run(nc, [arrays], core_ids=[0])
    return np.ascontiguousarray(r.results[0]["outT_dram"].T).reshape(BATCH, SEQ, D)
```
